# Optimizing a Trainium2 kernel written in Bass

```python
import numpy as np
import jax
import jax.numpy as jnp

def _softmax(x, axis=-1):
    return jax.nn.softmax(x, axis=axis)
def _gelu(x):
    return jax.nn.gelu(x, approximate=True)
def _silu(x):
    return jax.nn.silu(x)
def _sigmoid(x):
    return jax.nn.sigmoid(x)
def _layernorm(x, axis=-1, eps=1e-5):
    m = jnp.mean(x, axis=axis, keepdims=True)
    v = jnp.var(x, axis=axis, keepdims=True)
    return (x - m) / jnp.sqrt(v + eps)
def _scatter_add(tgt, idx, src, axis=0):
    return tgt.at[idx].add(src)
def _segment_sum(src, seg, n):
    return jax.ops.segment_sum(src, seg, n)

kernel_name = 'mk_metaformer_d1_conv_nhwc128_45d925'

def setup_inputs(seed: int = 0):
    np.random.seed(seed)
    _w = jnp.asarray
    def _rec_inputs():
        import jax
        import jax.numpy as jnp
        _gk = jax.random.key(seed)
        x = -0.000125 + 0.9999 * jax.random.normal(jax.random.fold_in(_gk, 1), (4, 256, 256, 128), jnp.float32)
        return x
    x = _rec_inputs()
    def _L0_conv_setup():
        import jax, jax.numpy as jnp
        import numpy as np
        EPS = 1e-05

        def _layernorm_hd(t, gamma, beta):
            mu = jnp.mean(t, axis=(-2, -1), keepdims=True)
            var = jnp.var(t, axis=(-2, -1), keepdims=True)
            return (t - mu) * jax.lax.rsqrt(var + EPS) * gamma + beta
        key = jax.random.key(seed)
        B, Hs, Ws, C = (4, 256, 256, 128)
        n_heads, head_dim = (4, C // 4)
        scale = C ** 2 / n_heads
        ks = jax.random.split(key, 4)
        X = jax.random.normal(ks[0], (B, Hs, Ws, C), dtype=jnp.float32)
        Wq = jax.random.normal(ks[1], (C, n_heads, head_dim), dtype=jnp.float32) / scale
        Wk = jax.random.normal(ks[2], (C, n_heads, head_dim), dtype=jnp.float32) / scale
        Wv = jax.random.normal(ks[3], (C, n_heads, head_dim), dtype=jnp.float32) / scale
        gamma_k = jnp.ones((n_heads, head_dim), dtype=jnp.float32)
        beta_k = jnp.zeros((n_heads, head_dim), dtype=jnp.float32)
        return {'X': X, 'Wq': Wq, 'Wk': Wk, 'Wv': Wv, 'gamma_k': gamma_k, 'beta_k': beta_k}
    _L0_conv_all = _L0_conv_setup()
    _L0_conv_in = {k: v for k, v in _L0_conv_all.items() if k in ('Wq', 'Wk', 'Wv', 'gamma_k', 'beta_k', )}
    del _L0_conv_all

    def _L0_ffn_setup():
        import jax, jax.numpy as jnp
        import numpy as np
        BN_EPS = 1e-05
        key = jax.random.key(seed)
        k1, k2, k3 = jax.random.split(key, 3)
        B, T, I, H = (64, 2048, 128, 128)
        x = jax.random.normal(k1, (B, T, I), dtype=jnp.float32)
        W = jax.random.normal(k2, (H, I), dtype=jnp.float32) * (1.0 / np.sqrt(I))
        V = jnp.linalg.qr(jax.random.normal(k3, (H, H), dtype=jnp.float32))[0]
        gamma = jnp.ones((H,), dtype=jnp.float32)
        beta = jnp.zeros((H,), dtype=jnp.float32)
        return {'x': x, 'W': W, 'V': V, 'gamma': gamma, 'beta': beta}
    _L0_ffn_all = _L0_ffn_setup()
    _L0_ffn_in = {k: v for k, v in _L0_ffn_all.items() if k in ('W', 'V', 'gamma', 'beta', )}
    del _L0_ffn_all

    return {
        "x": x,
        "L0_conv_Wq": _L0_conv_in["Wq"],
        "L0_conv_Wk": _L0_conv_in["Wk"],
        "L0_conv_Wv": _L0_conv_in["Wv"],
        "L0_conv_gamma_k": _L0_conv_in["gamma_k"],
        "L0_conv_beta_k": _L0_conv_in["beta_k"],
        "L0_ffn_W": _L0_ffn_in["W"],
        "L0_ffn_V": _L0_ffn_in["V"],
        "L0_ffn_gamma": _L0_ffn_in["gamma"],
        "L0_ffn_beta": _L0_ffn_in["beta"],
    }

def reference(x, L0_conv_Wq, L0_conv_Wk, L0_conv_Wv, L0_conv_gamma_k, L0_conv_beta_k, L0_ffn_W, L0_ffn_V, L0_ffn_gamma, L0_ffn_beta):
    import jax
    import jax.numpy as jnp
    def _L0_conv_ref(X, Wq, Wk, Wv, gamma_k, beta_k):
        import jax, jax.numpy as jnp
        import numpy as np
        EPS = 1e-05

        def _layernorm_hd(t, gamma, beta):
            mu = jnp.mean(t, axis=(-2, -1), keepdims=True)
            var = jnp.var(t, axis=(-2, -1), keepdims=True)
            return (t - mu) * jax.lax.rsqrt(var + EPS) * gamma + beta
        q = jnp.einsum('bxyc,chd->bxyhd', X, Wq)
        k = jnp.einsum('bxyc,chd->bxyhd', X, Wk)
        v = jnp.einsum('bxyc,chd->bxyhd', X, Wv)
        k = _layernorm_hd(k, gamma_k, beta_k)
        v = _layernorm_hd(v, gamma_k, beta_k)
        num_points = X.shape[1] * X.shape[2]
        kv = jnp.einsum('bxyhd,bxyhe->bhde', k, v)
        sa = jnp.einsum('bxyhd,bhde->bxyeh', q, kv)
        sa = (sa / num_points).reshape(X.shape)
        return sa

    def _L0_ffn_ref(x, W, V, gamma, beta):
        import jax, jax.numpy as jnp
        import numpy as np
        BN_EPS = 1e-05
        B, T, H = (x.shape[0], x.shape[1], W.shape[0])
        Wx = jnp.einsum('bti,hi->bth', x, W)
        flat = Wx.reshape(B * T, H)
        mean = jnp.mean(flat, axis=0)
        var = jnp.var(flat, axis=0)
        Wx = ((flat - mean) * jax.lax.rsqrt(var + BN_EPS) * gamma + beta).reshape(B, T, H)
        Vt = V.T

        def step(yt, wx_t):
            yt = jax.nn.sigmoid(wx_t + yt @ Vt)
            return (yt, yt)
        y0 = jnp.zeros((B, H), dtype=Wx.dtype)
        _, ys = jax.lax.scan(step, y0, jnp.swapaxes(Wx, 0, 1))
        return jnp.swapaxes(ys, 0, 1)

    def _gn(v, G=32, eps=1e-5):
        B_, H_, W_, C_ = v.shape
        g = v.reshape(B_, H_, W_, G, C_ // G)
        m = jnp.mean(g, axis=(1, 2, 4), keepdims=True)
        s = jnp.var(g, axis=(1, 2, 4), keepdims=True)
        return ((g - m) / jnp.sqrt(s + eps)).reshape(v.shape)

    def _ln_c(v, eps=1e-6):
        m = jnp.mean(v, axis=-1, keepdims=True)
        s = jnp.var(v, axis=-1, keepdims=True)
        return (v - m) / jnp.sqrt(s + eps)

    def _ln_t(v, eps=1e-5):
        m = jnp.mean(v, axis=-1, keepdims=True)
        s = jnp.var(v, axis=-1, keepdims=True)
        return (v - m) / jnp.sqrt(s + eps)

    def _to_tokens(v):
        B_, H_, W_, C_ = v.shape
        return v.reshape(B_, H_ * W_, C_)
    def _from_tokens(t, like):
        return t.reshape(like.shape)

    x = x + _L0_conv_ref(_ln_c(x), L0_conv_Wq, L0_conv_Wk, L0_conv_Wv, L0_conv_gamma_k, L0_conv_beta_k)
    t = _to_tokens(x)
    t = t + _L0_ffn_ref(_ln_t(t), L0_ffn_W, L0_ffn_V, L0_ffn_gamma, L0_ffn_beta)
    x = _from_tokens(t, x)
    return x


_drawn_inputs = setup_inputs


def setup_inputs(seed=0):
    import zlib

    import numpy as np

    out = dict(_drawn_inputs(seed))
    spreads = {'L0_conv_gamma_k': (1.0, 0.6),
     'L0_conv_beta_k': (0.0, 0.8),
     'L0_ffn_gamma': (1.0, 0.55),
     'L0_ffn_beta': (0.0, 0.41)}
    factors = {'L0_conv_Wq': 8.0, 'L0_conv_Wk': 8.0, 'L0_conv_Wv': 8.0}
    for name, (base, spread) in spreads.items():
        noise = np.random.default_rng([zlib.crc32(name.encode()), seed]).standard_normal(out[name].shape)
        drawn = base * np.exp(spread * noise) if base else spread * noise
        out[name] = jnp.asarray(drawn.astype(out[name].dtype))
    for name, factor in factors.items():
        out[name] = (out[name] * factor).astype(out[name].dtype)
    return out
```

```python
from contextlib import ExitStack

import concourse.bass as bass
from concourse import mybir

F32 = mybir.dt.float32
I32 = mybir.dt.int32
ALU = mybir.AluOpType
ACT = mybir.ActivationFunctionType
AX = mybir.AxisListType
P = 128


def metaformer_program(nc, x, Wq, Wk, Wv, gamma_k, beta_k, ffn_W, ffn_V, ffn_gamma, ffn_beta, out):
    B, HS, WS, C = x.shape
    N = HS * WS
    HEADS, HD = Wq.shape[1], Wq.shape[2]
    CHUNK = N // P
    GT = 16
    QT = 4
    NQ = GT // QT
    RING = 4
    GB = CHUNK // GT
    BODIES = GB // RING
    NCOL = B * P
    BT = 16
    HT = BT // 2
    CB = CHUNK // BT
    LN_C_EPS, HD_EPS, LN_T_EPS, BN_EPS = 1e-6, 1e-5, 1e-5, 1e-5
    SETTLED = 2.0 ** -20
    assert C == P and HEADS * HD == P and B * C == 512 and CB * BT == CHUNK

    x_g = x.rearrange("b h w c -> b (h w c)").rearrange("b (p f) -> b p f", p=P)
    out_g = out.rearrange("b h w c -> b (h w c)").rearrange("b (p f) -> p b f", p=P)
    x2_dram = nc.dram_tensor("x2_scratch", [CHUNK // HT, P, B, HT * C], F32, kind="Internal").ap()

    with ExitStack() as ctx:
        def sb(name, shape, dt=F32):
            return ctx.enter_context(nc.sbuf_tensor(name, shape, dt))

        def sem(name):
            return ctx.enter_context(nc.semaphore(name))

        xg = sb("xg", [P, RING, GT * C])
        x2g = sb("x2g", [P, RING, GT * C])
        xs = sb("xs", [P, 2, GT, C + 2])
        xT = sb("xT", [P, 4, QT * P])
        xn = sb("xn", [P, 4, B, C])
        y = sb("y", [P, 4, NCOL])
        entry = sb("entry", [P, NCOL])
        entry_next = sb("entry_next", [P, NCOL])
        entry_diff = sb("entry_diff", [P, NCOL])
        diff_max = sb("diff_max", [P, 1])
        diff_all = sb("diff_all", [P, 1])
        rounds_limit = sb("rounds_limit", [P, 1], I32)
        r1_all = sb("r1_all", [P, B * CHUNK + GT])
        r2_flat = sb("r2_flat", [P, B * CHUNK + GT])
        r2_all = sb("r2_all", [P, B, CHUNK + BT])
        r1_now = sb("r1_now", [P, 2, GT])
        x_stats = sb("x_stats", [P, GT, 6])
        z_stats = sb("z_stats", [P, GT, 6])
        mean_gap = sb("mean_gap", [P, GT, 1])
        sum_sq = sb("sum_sq", [P, GT, 1])
        gap_sq = sb("gap_sq", [P, GT, 1])
        var_in = sb("var_in", [P, 2, GT, 3])
        var_eps = sb("var_eps", [P, GT, 3])
        rstd = sb("rstd", [P, GT, 3])
        kv_scale = sb("kv_scale", [P, GT, 1])
        minus_half = sb("minus_half", [P, GT, 3])
        ident = sb("ident", [P, P])
        center = sb("center", [P, P])
        zeros = sb("zeros", [P, C + 2])
        w_in = sb("w_in", [P, 5, P])
        gamma_row = sb("gamma_row", [P, P])
        beta_row = sb("beta_row", [1, P])
        bn_gamma = sb("bn_gamma", [P, 1])
        bn_beta = sb("bn_beta", [P, 1])
        w_kv = sb("w_kv", [P, 2 * P])
        w_c = sb("w_c", [P, 3, P])
        w_mean = sb("w_mean", [P, 3])
        w_kvg = sb("w_kvg", [P, 2, P])
        w_qT = sb("w_qT", [P, P])
        f_c = sb("f_c", [P, P])
        f_cT = sb("f_cT", [P, P])
        f_scaled = sb("f_scaled", [P, P])
        f_scaledT = sb("f_scaledT", [P, P])
        v_T = sb("v_T", [P, P])
        gram = sb("gram", [P, B, C + 2])
        gram2 = sb("gram2", [P, C + 1])
        gram_v = sb("gram_v", [P, B, P])
        rows = sb("rows", [1, 2, B, P])
        kv_heads = sb("kv_heads", [P, B, P])
        m_all = sb("m_all", [P, B * P])
        bn_prod = sb("bn_prod", [P, P])
        bn_cols = sb("bn_cols", [P, 8])

        pT = ctx.enter_context(nc.psum_tensor("pT", [P, 2, 512], F32))
        pZ = ctx.enter_context(nc.psum_tensor("pZ", [P, 2, 2, 512], F32))
        pG = ctx.enter_context(nc.psum_tensor("pG", [P, 512], F32))
        pM = ctx.enter_context(nc.psum_tensor("pM", [P, 512], F32))

        w_loaded = sem("w_loaded")
        consts_done, ident_made = sem("consts_done"), sem("ident_made")
        setup_pe, setup_dve, dve_chain, setup_done = sem("setup_pe"), sem("setup_dve"), sem("dve_chain"), sem("setup_done")
        bn_var, bn_rstd, r2_placed = sem("bn_var"), sem("bn_rstd"), sem("r2_placed")
        x_in = [sem(f"x_in{j}") for j in range(RING)]
        a_T, a_xT, a_z, a_z_read = sem("a_T"), sem("a_xT"), sem("a_z"), sem("a_z_read")
        a_small, a_var, a_var_read = sem("a_small"), sem("a_var"), sem("a_var_read")
        a_pool, a_xs, a_gram, gram_saved = sem("a_pool"), sem("a_xs"), sem("a_gram"), sem("gram_saved")
        b_T, b_xT, b_u, b_x2 = sem("b_T"), sem("b_xT"), sem("b_u"), sem("b_x2")
        b_small, b_var, b_var_read = sem("b_small"), sem("b_var"), sem("b_var_read")
        b_pool, b_xs, b_gram, b_r1 = sem("b_pool"), sem("b_xs"), sem("b_gram"), sem("b_r1")
        x2_stored = [sem(f"x2_stored{j}") for j in range(RING)]
        x2_in = [sem(f"x2_in{j}") for j in range(2)]
        out_stored = [sem(f"out_stored{j}") for j in range(2)]
        c_xn, c_T, c_xT, c_pre, c_w, c_y = sem("c_xn"), sem("c_T"), sem("c_xT"), sem("c_pre"), sem("c_w"), sem("c_y")
        c_back, c_out = sem("c_back"), sem("c_out")
        c_chain, entry_set, diff_ready, diff_reduced, verdict = (
            sem("c_chain"), sem("entry_set"), sem("diff_ready"), sem("diff_reduced"), sem("verdict"))

        PRIMED = 1

        def tile(buf, j, t):
            return buf[:, j, t * C:(t + 1) * C]

        def quad_f(ap, c):
            return ap[:, c * QT * C:(c + 1) * QT * C].rearrange("p (t c) -> p t c", c=C)

        def wait_pos(eng, s, value):
            if not (isinstance(value, int) and value <= 0):
                eng.wait_ge(s, value)

        passed = {e: sem(f"passed_{e}") for e in ("sp", "pe", "act", "dve", "pool")}

        def wait_alone(eng, who, s, value):
            eng.wait_ge(s, value)
            eng.sem_inc(passed[who], 1)

        block = ctx.enter_context(nc.Block())

        @block.sync
        def _(sp):
            def load_x(b, g, j):
                sp.dma_start(xg[:, j, :], x_g[b, :, bass.ds(g * (GT * C), GT * C)]).then_inc(x_in[j], 16)

            for n, w in enumerate((Wq, Wk, Wv)):
                sp.dma_start(w_in[:, n, :], w.rearrange("c h d -> c (h d)")).then_inc(w_loaded, 16)
            sp.dma_start(w_in[:, 3, :], ffn_W).then_inc(w_loaded, 16)
            sp.dma_start(w_in[:, 4, :], ffn_V).then_inc(w_loaded, 16)
            sp.dma_start(gamma_row[:, :], gamma_k.rearrange("h d -> (h d)").partition_broadcast(P)).then_inc(w_loaded, 16)
            sp.dma_start(beta_row[:, :], beta_k.rearrange("(a h) d -> a (h d)", a=1)).then_inc(w_loaded, 16)
            sp.dma_start(bn_gamma[:, :], ffn_gamma.rearrange("(p a) -> p a", a=1)).then_inc(w_loaded, 16)
            sp.dma_start(bn_beta[:, :], ffn_beta.rearrange("(p a) -> p a", a=1)).then_inc(w_loaded, 16)

            for j in range(RING):
                load_x(0, j, j)

            def refill_a(b, i):
                for j in range(RING):
                    wait_alone(sp, "sp", a_gram, b * (GB * NQ) + i * (RING * NQ) + (j + 1 - RING) * NQ + PRIMED)
                    load_x(b, i * RING + j, j)

            with sp.Fori(1, BODIES) as i:
                refill_a(0, i)
            with sp.Fori(1, B) as b:
                with sp.Fori(0, BODIES) as i:
                    refill_a(b, i)
            for j in range(RING):
                sp.wait_ge(a_gram, B * GB * NQ + (j + 1 - RING) * NQ + PRIMED)
                load_x(0, j, j)

            def store_x2(b, i, j):
                sp.dma_start(
                    x2_dram[bass.ds((i * RING + j) * 2, 2), :, b, :].rearrange("k p f -> p k f"),
                    x2g[:, j, :].rearrange("p (k f) -> p k f", k=2)).then_inc(x2_stored[j], 16)

            def step_b(b, i, load):
                for j in range(RING):
                    wait_alone(sp, "sp", b_gram, b * (GB * NQ) + i * (RING * NQ) + (j + 1) * NQ + PRIMED)
                    load(j)
                    store_x2(b, i, j)

            with sp.Fori(0, B - 1) as b:
                with sp.Fori(0, BODIES - 1) as i:
                    step_b(b, i, lambda j: load_x(b, (i + 1) * RING + j, j))
                step_b(b, BODIES - 1, lambda j: load_x(b + 1, j, j))
            with sp.Fori(0, BODIES - 1) as i:
                step_b(B - 1, i, lambda j: load_x(B - 1, (i + 1) * RING + j, j))
            step_b(B - 1, BODIES - 1, lambda j: load_x(0, j, j) if j < 2 else None)
            for j in range(RING):
                sp.wait_ge(x2_stored[j], 16 * (B * BODIES + PRIMED))

            def load_x2(k, half):
                sp.dma_start(xg[:, 2 * half:2 * half + 2, :].rearrange("p a f -> p (a f)"),
                             x2_dram[bass.ds(k * 2 + half, 1), :, :, :].rearrange("a p b f -> p (a b f)")
                             ).then_inc(x2_in[half], 16)

            def step_c(n, k, k_next):
                for half in range(2):
                    wait_alone(sp, "sp", c_out, n * BT + (half + 1) * HT)
                    sp.dma_start(out_g[:, :, bass.ds(k * (BT * C) + half * (HT * C), HT * C)],
                                 x2g[:, 2 * half:2 * half + 2, :].rearrange("p a (b f) -> p (a b) f", b=2)
                                 ).then_inc(out_stored[half], 16)
                    load_x2(k_next, half)

            for j in range(2):
                sp.wait_ge(x_in[j], 16 * (2 * B * BODIES + 1))
            sp.wait_ge(b_T, (B * GB + 1) * NQ + 2)
            sp.wait_ge(b_x2, (B * GB + 1) * NQ)
            load_x2(CB - 1, 0)
            load_x2(CB - 1, 1)
            step_c(0, CB - 1, 0)
            limit = sp.alloc_register("sp_limit")
            sp.reg_mov(limit, 1)
            with sp.Fori(0, limit) as r:
                with sp.Fori(0, CB - 1) as k:
                    step_c(r * CB + k + 1, k, k + 1)
                step_c(r * CB + CB, CB - 1, 0)
                for half in range(2):
                    wait_alone(sp, "sp", out_stored[half], r * (16 * CB) + 16 * (CB + 1))
                    wait_alone(sp, "sp", x2_in[half], r * (16 * CB) + 16 * (CB + 2))
                wait_alone(sp, "sp", verdict, r + 1)
                sp.reg_load(limit, rounds_limit[0:1, 0:1])

        @block.tensor
        def _(pe):
            pe.wait_ge(w_loaded, 16 * 9)
            pe.wait_ge(consts_done, 1)
            for n in range(3):
                last = nc.tensor.matmul(pM[:, n * P:(n + 1) * P], center[:, :], w_in[:, n, :], start=True, stop=True)
            last.then_inc(setup_pe, 1)
            nc.tensor.transpose(pT[:, 0, 0:P], w_in[:, 4, :], ident[:, :]).then_inc(setup_pe, 1)
            pe.wait_ge(setup_dve, 1)
            nc.tensor.transpose(pT[:, 1, 0:P], w_c[:, 0, :], ident[:, :]).then_inc(setup_pe, 1)
            pe.wait_ge(setup_dve, 2)
            nc.tensor.transpose(pG[:, 0:P], f_c[:, :], ident[:, :]).then_inc(setup_pe, 1)
            pe.wait_ge(setup_done, 1)

            def transposes(src, s_T, s_xT, j, c, q, first=False, loads=None):
                if loads is not None:
                    pe.wait_ge(x_in[j], loads)
                if not first:
                    pe.wait_ge(s_xT, q - 1)
                for t in range(QT):
                    last = nc.tensor.transpose(pT[:, c % 2, t * P:(t + 1) * P], tile(src, j, c * QT + t), ident[:, :])
                last.then_inc(s_T, 1)

            def group_a(j, q0, first=False):
                for c in range(NQ):
                    q = q0 + c
                    pe.wait_ge(a_xT, q + 1)
                    if not (first and c < 2):
                        pe.wait_ge(a_z_read, q - 1)
                    for t in range(QT):
                        last = nc.tensor.matmul(pZ[:, c % 2, t // 2, (t % 2) * 2 * P:(t % 2 + 1) * 2 * P],
                                                xT[:, c % 4, t * P:(t + 1) * P], w_kv[:, :], start=True, stop=True)
                    last.then_inc(a_z, 1)
                    if c < 2:
                        transposes(xg, a_T, a_xT, j, c + 2, q + 2)

            def gram_quad(s_xs, s_gram, src, ring, width, j, c, need):
                pe.wait_ge(s_xs, need)
                for t in range(QT):
                    last = nc.tensor.matmul(pG[:, 0:width], tile(src, j, c * QT + t),
                                            xs[:, ring, c * QT + t, 0:width], start=False, stop=False,
                                            skip_group_check=True)
                last.then_inc(s_gram, 1)

            def open_gram(width):
                return nc.tensor.matmul(pG[:, 0:width], zeros[:, 0:P], zeros[:, 0:width], start=True, stop=False,
                                        skip_group_check=True)

            transposes(xg, a_T, a_xT, 0, 0, 0, first=True, loads=16)
            transposes(xg, a_T, a_xT, 0, 1, 1, first=True)
            group_a(0, 0, first=True)
            transposes(xg, a_T, a_xT, 1, 0, NQ, loads=16)
            transposes(xg, a_T, a_xT, 1, 1, NQ + 1)
            open_gram(C + 2).then_inc(a_gram, PRIMED)
            with pe.Fori(0, B) as b:
                pe.wait_ge(gram_saved, b + PRIMED)
                open_gram(C + 2)
                with pe.Fori(0, BODIES) as i:
                    n = pe.snap(b * BODIES + i)
                    q0 = pe.snap(n * (RING * NQ))
                    for j in range(RING):
                        j1, j2 = (j + 1) % RING, (j + 2) % RING
                        group_a(j1, q0 + (j + 1) * NQ)
                        for c in range(NQ):
                            if c == NQ - 1:
                                transposes(xg, a_T, a_xT, j2, 0, q0 + (j + 2) * NQ, loads=n * 16 + 16 * (1 + (j + 2) // RING))
                                transposes(xg, a_T, a_xT, j2, 1, q0 + (j + 2) * NQ + 1)
                            gram_quad(a_xs, a_gram, xg, j % 2, C + 2, j, c, q0 + j * NQ + c + 1)

            pe.wait_ge(gram_saved, B + PRIMED)
            pe.wait_ge(a_xT, (B * GB + 1) * NQ + 2)
            for b in range(B):
                last = nc.tensor.matmul(pM[:, b * P:(b + 1) * P], gram[:, b, 0:C], w_kvg[:, 1, :], start=True, stop=True)
            last.then_inc(setup_pe, 1)
            for n in range(2):
                for b in range(B):
                    last = nc.tensor.matmul(pT[0:1, n, b * P:(b + 1) * P], gram[:, b, C + n:C + n + 1],
                                            w_kvg[:, n, :], start=True, stop=True)
            last.then_inc(setup_pe, 1)
            pe.wait_ge(setup_dve, 3)
            nc.tensor.matmul(pZ[:, 0, 0, :], w_kvg[:, 0, :], gram_v[:, :, :].rearrange("p b c -> p (b c)"),
                             start=True, stop=False, skip_group_check=True)
            for b in range(B):
                nc.tensor.matmul(pZ[:, 0, 0, b * P:(b + 1) * P], rows[0:1, 0, b, :], beta_row[:, :],
                                 start=False, stop=False, skip_group_check=True)
            nc.tensor.matmul(pZ[:, 0, 0, :], beta_row[:, :], rows[0:1, 1, :, :].rearrange("a b c -> a (b c)"),
                             start=False, stop=True, skip_group_check=True).then_inc(setup_pe, 1)
            pe.wait_ge(setup_dve, 4)
            nc.tensor.matmul(pM[:, :], w_qT[:, :], kv_heads[:, :, :].rearrange("p b c -> p (b c)"),
                             start=True, stop=True).then_inc(setup_pe, 1)
            pe.wait_ge(setup_dve, 5)

            def group_b(j, q0, m_now, first=False):
                for c in range(NQ):
                    q = q0 + c
                    pe.wait_ge(b_xT, q + 1)
                    if not (first and c < 2):
                        pe.wait_ge(b_x2, q - 1)
                    for t in range(QT):
                        last = nc.tensor.matmul(pZ[:, c % 2, 0, t * P:(t + 1) * P],
                                                xT[:, c % 4, t * P:(t + 1) * P], m_now, start=True, stop=True)
                    last.then_inc(b_u, 1)
                    if c < 2:
                        transposes(xg, b_T, b_xT, j, c + 2, q + 2)

            A_LOADS = 16 * B * BODIES
            transposes(xg, b_T, b_xT, 0, 0, 0, first=True, loads=A_LOADS + 16)
            transposes(xg, b_T, b_xT, 0, 1, 1, first=True)
            group_b(0, 0, m_all[:, 0:P], first=True)
            transposes(xg, b_T, b_xT, 1, 0, NQ, loads=A_LOADS + 16)
            transposes(xg, b_T, b_xT, 1, 1, NQ + 1)
            open_gram(C + 1).then_inc(b_gram, PRIMED)
            with pe.Fori(0, B) as b:
                def body_b(i, b_next):
                    n = pe.snap(b * BODIES + i)
                    q0 = pe.snap(n * (RING * NQ))
                    for j in range(RING):
                        j1, j2 = (j + 1) % RING, (j + 2) % RING
                        bb = b if j < RING - 1 else b_next
                        group_b(j1, q0 + (j + 1) * NQ, m_all[:, bass.ds(bb * P, P)])
                        for c in range(NQ):
                            if c == NQ - 1:
                                transposes(xg, b_T, b_xT, j2, 0, q0 + (j + 2) * NQ,
                                           loads=n * 16 + A_LOADS + 16 * (1 + (j + 2) // RING))
                                transposes(xg, b_T, b_xT, j2, 1, q0 + (j + 2) * NQ + 1)
                            gram_quad(b_xs, b_gram, x2g, j % 2, C + 1, j, c, q0 + j * NQ + c + 1)

                with pe.Fori(0, BODIES - 1) as i:
                    body_b(i, b)
                body_b(BODIES - 1, pe.snap((b + 1) % B))

            pe.wait_ge(gram_saved, B + 1 + PRIMED)
            nc.tensor.matmul(pM[:, 0:P], f_cT[:, :], gram2[:, 0:C], start=True, stop=True)
            nc.tensor.matmul(pM[:, P:P + 1], f_cT[:, :], gram2[:, C:C + 1], start=True, stop=True).then_inc(setup_pe, 1)
            pe.wait_ge(setup_dve, 6)
            nc.tensor.transpose(pM[:, 0:P], f_scaled[:, :], ident[:, :]).then_inc(setup_pe, 1)
            pe.wait_ge(setup_dve, 7)
            pe.wait_ge(b_xT, (B * GB + 1) * NQ + 2)

            def forward(s, ring):
                pe.wait_ge(c_xn, s + 1)
                wait_pos(pe, c_xT, s - 1)
                for b in range(B):
                    last = nc.tensor.transpose(pT[:, ring % 2, b * P:(b + 1) * P], xn[:, ring % 4, b, :], ident[:, :])
                last.then_inc(c_T, 1)

            def project(s, ring):
                pe.wait_ge(c_xT, s + 1)
                nc.tensor.matmul(pZ[:, 0, ring % 2, :], f_scaledT[:, :], xT[:, ring % 2, :], start=True, stop=False,
                                 skip_group_check=True).then_inc(c_w, 1)

            def recur(s, ring):
                nc.tensor.matmul(pZ[:, 0, ring % 2, :], v_T[:, :], y[:, (ring + 3) % 4, :], start=False, stop=True,
                                 skip_group_check=True).then_inc(c_pre, 1)

            def back(s, ring):
                pe.wait_ge(c_y, s + 1)
                wait_pos(pe, c_out, s - 1)
                for b in range(B):
                    last = nc.tensor.transpose(pZ[:, 1, ring % 2, b * P:(b + 1) * P], y[:, ring % 4, b * P:(b + 1) * P],
                                               ident[:, :])
                last.then_inc(c_back, 1)

            def body_c(n, enter):
                s0 = n * BT if isinstance(n, int) else pe.snap(n * BT)
                for t in range(BT):
                    if t or not enter:
                        pe.wait_ge(c_y, s0 + t)
                    recur(s0 + t, t)
                    project(s0 + t + 1, t + 1)
                    forward(s0 + t + 2, t + 2)
                    back(s0 + t, t)

            forward(0, 0)
            forward(1, 1)
            project(0, 0)
            pe.wait_ge(entry_set, 1)
            body_c(0, True)
            limit = pe.alloc_register("pe_limit")
            pe.reg_mov(limit, 1)
            with pe.Fori(0, limit) as r:
                wait_alone(pe, "pe", entry_set, r + 2)
                with pe.Fori(0, CB) as k:
                    body_c(r * CB + k + 1, False)
                wait_alone(pe, "pe", verdict, r + 1)
                pe.reg_load(limit, rounds_limit[0:1, 0:1])

        @block.scalar
        def _(act):
            def copy_quad(s_T, s_z, s_xT, q, c, first=False):
                act.wait_ge(s_T, q + 1)
                if not first:
                    act.wait_ge(s_z, q - 3)
                nc.scalar.activation(xT[:, c % 4, :], pT[:, c % 2, :], ACT.Copy).then_inc(s_xT, 1)

            def body_ab(n, s_T, s_z, s_xT):
                q0 = act.snap(n * (RING * NQ))
                for k in range(RING * NQ):
                    q = NQ + 2 + k
                    copy_quad(s_T, s_z, s_xT, q0 + q, q)

            for q in range(NQ + 2):
                copy_quad(a_T, a_z, a_xT, q, q, first=q < 4)
            with act.Fori(0, B) as b:
                with act.Fori(0, BODIES) as i:
                    body_ab(b * BODIES + i, a_T, a_z, a_xT)
                act.wait_ge(a_gram, b * (GB * NQ) + GB * NQ + PRIMED)
                nc.scalar.activation(gram[:, bass.ds(b, 1), :].rearrange("p a c -> p (a c)"), pG[:, 0:C + 2],
                                     ACT.Copy).then_inc(gram_saved, 1)

            act.wait_ge(setup_dve, 5)
            for q in range(NQ + 2):
                copy_quad(b_T, b_u, b_xT, q, q, first=q < 4)
            with act.Fori(0, B * BODIES) as n:
                body_ab(n, b_T, b_u, b_xT)
            act.wait_ge(b_gram, B * GB * NQ + PRIMED)
            nc.scalar.activation(gram2[:, :], pG[:, 0:C + 1], ACT.Copy).then_inc(gram_saved, 1)

            def body_c(n):
                s0 = n * BT if isinstance(n, int) else act.snap(n * BT)
                for t in range(BT):
                    act.wait_ge(c_pre, s0 + t + 1)
                    nc.scalar.activation(y[:, t % 4, :], pZ[:, 0, t % 2, :], ACT.Sigmoid,
                                         bias=bn_cols[:, 7:8]).then_inc(c_y, 1)

            act.wait_ge(setup_dve, 7)
            body_c(0)
            limit = act.alloc_register("act_limit")
            act.reg_mov(limit, 1)
            with act.Fori(0, limit) as r:
                with act.Fori(0, CB) as k:
                    body_c(r * CB + k + 1)
                wait_alone(act, "act", verdict, r + 1)
                act.reg_load(limit, rounds_limit[0:1, 0:1])

        @block.vector
        def _(dve):
            chain = [0]

            def link(ins):
                chain[0] += 1
                ins.then_inc(dve_chain, 1)
                dve.wait_ge(dve_chain, chain[0])

            dve.wait_ge(w_loaded, 16 * 9)
            dve.wait_ge(consts_done, 1)
            dve.wait_ge(setup_pe, 1)
            nc.vector.tensor_copy(w_kv[:, 0:2 * P:2], pM[:, P:2 * P])
            nc.vector.tensor_copy(w_kv[:, 1:2 * P:2], pM[:, 2 * P:3 * P])
            nc.vector.tensor_copy(w_c[:, :, :].rearrange("p a b -> p (a b)"), pM[:, 0:3 * P]).then_inc(setup_dve, 1)
            dve.wait_ge(setup_dve, 1)
            link(nc.vector.tensor_reduce(w_mean[:, :], w_c[:, :, :], AX.X, ALU.add))
            link(nc.vector.tensor_scalar(w_mean[:, :], w_mean[:, :], 1.0 / P, None, ALU.mult))
            for n in range(2):
                nc.vector.scalar_tensor_tensor(w_kvg[:, n, :], w_c[:, 1 + n, :], w_mean[:, 1 + n:2 + n], gamma_row[:, :],
                                               ALU.subtract, ALU.mult)
            link(nc.vector.tensor_reduce(bn_cols[:, 0:1], w_in[:, 3, :], AX.X, ALU.add))
            link(nc.vector.tensor_scalar(bn_cols[:, 1:2], bn_cols[:, 0:1], 1.0 / P, None, ALU.mult))
            nc.vector.tensor_scalar(f_c[:, :], w_in[:, 3, :], bn_cols[:, 1:2], None, ALU.subtract).then_inc(setup_dve, 1)
            dve.wait_ge(setup_pe, 3)
            nc.vector.tensor_copy(v_T[:, :], pT[:, 0, 0:P])
            nc.vector.tensor_copy(w_qT[:, :], pT[:, 1, 0:P])
            dve.wait_ge(setup_pe, 4)
            nc.vector.tensor_copy(f_cT[:, :], pG[:, 0:P]).then_inc(setup_done, 1)
            nc.vector.memset(kv_heads[:, :, :], 0.0)
            nc.vector.memset(entry_next[:, :], 0.0)
            nc.vector.memset(y[:, 3, :], 0.0).then_inc(entry_set, 1)
            nc.vector.memset(entry[:, :], 0.0).then_inc(gram_saved, PRIMED)

            def var_of_x(s_small, par, base):
                dve.wait_ge(s_small, base + 1)
                nc.vector.tensor_tensor(mean_gap[:, :, :], x_stats[:, :, 1:2], x_stats[:, :, 4:5], ALU.subtract)
                nc.vector.tensor_tensor(sum_sq[:, :, :], x_stats[:, :, 2:3], x_stats[:, :, 5:6],
                                        ALU.add).then_inc(s_small, 1)
                dve.wait_ge(s_small, base + 2)
                nc.vector.scalar_tensor_tensor(gap_sq[:, :, :], mean_gap[:, :, :], C / 4.0, mean_gap[:, :, :],
                                               ALU.mult, ALU.mult).then_inc(s_small, 1)
                dve.wait_ge(s_small, base + 3)
                return nc.vector.tensor_tensor(var_in[:, par, :, 0:1], sum_sq[:, :, :], gap_sq[:, :, :], ALU.add)

            def group_a(j, par, q0, g, loads, first=False):
                dve.wait_ge(x_in[j], loads)
                for t in range(GT):
                    last = nc.vector.bn_stats(x_stats[:, t, :], tile(xg, j, t))
                last.then_inc(a_small, 1)
                if not first:
                    dve.wait_ge(a_var, g)
                for c in range(NQ):
                    dve.wait_ge(a_z, q0 + c + 1)
                    for t in range(QT):
                        last = nc.vector.bn_stats(z_stats[:, c * QT + t, :],
                                                  pZ[:, c % 2, t // 2, (t % 2) * 2 * P:(t % 2 + 1) * 2 * P])
                    last.then_inc(a_z_read, 1)
                if not first:
                    dve.wait_ge(a_var_read, g - 2 + 1 + PRIMED)
                var_of_x(a_small, par, g * 4).then_inc(a_small, 1)
                dve.wait_ge(a_small, g * 4 + 4)
                dve.wait_ge(a_z_read, q0 + NQ)
                nc.vector.scalar_tensor_tensor(
                    var_in[:, par, :, 1:3], var_in[:, par, :, 0:1].to_broadcast([P, GT, 2]), HD_EPS,
                    z_stats[:, :, 2:6:3], ALU.mult, ALU.add).then_inc(a_var, 1)

            group_a(0, 0, 0, 0, 16, first=True)
            with dve.Fori(0, B * BODIES) as n:
                q0 = dve.snap(n * (RING * NQ))
                g0 = dve.snap(n * RING)
                for j in range(RING):
                    group_a((j + 1) % RING, (j + 1) % 2, q0 + (j + 1) * NQ, g0 + (j + 1), n * 16 + 16 * (1 + (j + 1) // RING))

            dve.wait_ge(setup_pe, 5)
            nc.vector.tensor_copy(gram_v[:, :, :].rearrange("p b c -> p (b c)"), pM[:, :])
            dve.wait_ge(setup_pe, 6)
            nc.vector.scalar_tensor_tensor(rows[:, 0, :, :], beta_row[:, :].unsqueeze(1).to_broadcast([1, B, P]), float(N),
                                           pT[0:1, 0, :].rearrange("a (b c) -> a b c", b=B), ALU.mult, ALU.add)
            nc.vector.tensor_copy(rows[:, 1, :, :], pT[0:1, 1, :].rearrange("a (b c) -> a b c", b=B)).then_inc(setup_dve, 1)
            dve.wait_ge(setup_pe, 7)
            for h in range(HEADS):
                hs = slice(h * HD, (h + 1) * HD)
                last = nc.vector.tensor_scalar(kv_heads[hs, :, hs],
                                               pZ[:, 0, 0, :].rearrange("p (b c) -> p b c", b=B)[hs, :, hs],
                                               1.0 / N, None, ALU.mult)
            last.then_inc(setup_dve, 1)
            dve.wait_ge(setup_pe, 8)
            nc.vector.tensor_copy(m_all[:, :].rearrange("p (b e h) -> p b h e", b=B, h=HEADS),
                                  pM[:, :].rearrange("p (b h e) -> p b h e", b=B, h=HEADS)).then_inc(setup_dve, 1)

            def group_b(j, par, q0, g, loads, stores, first=False):
                nc.vector.tensor_copy(r1_now[:, par, :], r1_all[:, bass.ds(g * GT, GT)]).then_inc(b_r1, 1)
                dve.wait_ge(b_r1, g + 1)
                dve.wait_ge(x_in[j], loads)
                dve.wait_ge(x2_stored[j], stores)
                if not first:
                    dve.wait_ge(b_var, g)

                def stats(c):
                    dve.wait_ge(b_x2, q0 + c + 1)
                    for t in range(QT):
                        last = nc.vector.bn_stats(x_stats[:, c * QT + t, :], tile(x2g, j, c * QT + t))
                    return last

                for c in range(NQ):
                    dve.wait_ge(b_u, q0 + c + 1)
                    for t in range(QT):
                        tt = c * QT + t
                        last = nc.vector.scalar_tensor_tensor(
                            tile(x2g, j, tt), pZ[:, c % 2, 0, t * P:(t + 1) * P], r1_now[:, par, tt:tt + 1],
                            tile(xg, j, tt), ALU.mult, ALU.add)
                    last.then_inc(b_x2, 1)
                    if c:
                        stats(c - 1)
                stats(NQ - 1).then_inc(b_small, 1)
                if not first:
                    dve.wait_ge(b_var_read, g - 2 + 1 + PRIMED)
                var_of_x(b_small, par, g * 3).then_inc(b_var, 1)

            A_LOADS = 16 * B * BODIES
            dve.wait_ge(a_pool, 2 * (B * GB + 1))
            group_b(0, 0, 0, 0, A_LOADS + 16, 16 * PRIMED, first=True)
            with dve.Fori(0, B * BODIES) as n:
                q0 = dve.snap(n * (RING * NQ))
                g0 = dve.snap(n * RING)
                for j in range(RING):
                    body = (j + 1) // RING
                    group_b((j + 1) % RING, (j + 1) % 2, q0 + (j + 1) * NQ, g0 + (j + 1),
                            n * 16 + A_LOADS + 16 * (1 + body), n * 16 + 16 * (body + PRIMED))

            dve.wait_ge(setup_pe, 9)
            link(nc.vector.tensor_tensor(bn_prod[:, :], pM[:, 0:P], f_c[:, :], ALU.mult))
            nc.vector.tensor_scalar(bn_cols[:, 3:4], pM[:, P:P + 1], 1.0 / (B * N), None, ALU.mult)
            link(nc.vector.tensor_reduce(bn_cols[:, 2:3], bn_prod[:, :], AX.X, ALU.add))
            link(nc.vector.tensor_tensor(bn_cols[:, 4:5], bn_cols[:, 3:4], bn_cols[:, 3:4], ALU.mult))
            link(nc.vector.scalar_tensor_tensor(bn_cols[:, 5:6], bn_cols[:, 2:3], 1.0 / (B * N), bn_cols[:, 4:5],
                                                ALU.mult, ALU.subtract))
            nc.vector.tensor_scalar(bn_cols[:, 5:6], bn_cols[:, 5:6], BN_EPS, None, ALU.add).then_inc(bn_var, 1)
            dve.wait_ge(bn_rstd, 1)
            link(nc.vector.tensor_tensor(bn_cols[:, 0:1], bn_cols[:, 6:7], bn_gamma[:, :], ALU.mult))
            link(nc.vector.tensor_tensor(bn_cols[:, 1:2], bn_cols[:, 3:4], bn_cols[:, 0:1], ALU.mult))
            nc.vector.tensor_tensor(bn_cols[:, 7:8], bn_beta[:, :], bn_cols[:, 1:2], ALU.subtract)
            nc.vector.tensor_scalar(f_scaled[:, :], f_c[:, :], bn_cols[:, 0:1], None, ALU.mult).then_inc(setup_dve, 1)
            dve.wait_ge(setup_pe, 10)
            nc.vector.tensor_copy(f_scaledT[:, :], pM[:, 0:P]).then_inc(setup_dve, 1)

            x2_half = xg[:, :, :].rearrange("p (h two) (b t c) -> p h (two b) t c", two=2, b=2, c=C)
            out_half = x2g[:, :, :].rearrange("p (h two) (b t c) -> p h (two b) t c", two=2, b=2, c=C)

            def take_forward(s, ring):
                dve.wait_ge(c_T, s + 1)
                wait_pos(dve, c_w, s - 1)
                nc.vector.tensor_copy(xT[:, ring % 2, :], pT[:, ring % 2, :]).then_inc(c_xT, 1)

            def body_c(n):
                s0 = n * BT if isinstance(n, int) else dve.snap(n * BT)
                for t in range(BT):
                    half = t // HT
                    take_forward(s0 + t + 2, t + 2)
                    if t % HT == 0:
                        wait_pos(dve, out_stored[half], n * 16)
                    dve.wait_ge(c_back, s0 + t + 1)
                    nc.vector.tensor_tensor(out_half[:, half, :, t % HT, :],
                                            pZ[:, 1, t % 2, :].rearrange("p (b c) -> p b c", b=B),
                                            x2_half[:, half, :, t % HT, :], ALU.add).then_inc(c_out, 1)

            by_batch = lambda ap: ap.rearrange("p (b c) -> p b c", b=B)

            dve.wait_ge(b_xs, (B * GB + 1) * NQ)
            dve.wait_ge(b_xT, (B * GB + 1) * NQ + 2)
            take_forward(0, 0)
            take_forward(1, 1)
            body_c(0)
            link(nc.vector.tensor_copy(by_batch(entry_next[:, :])[:, :, 1:P], by_batch(y[:, 3, :])[:, :, 0:P - 1]))
            nc.vector.tensor_copy(entry[:, :], entry_next[:, :])
            nc.vector.tensor_copy(y[:, 3, :], entry_next[:, :]).then_inc(entry_set, 1)
            limit = dve.alloc_register("dve_limit")
            dve.reg_mov(limit, 1)
            with dve.Fori(0, limit) as r:
                with dve.Fori(0, CB) as k:
                    body_c(r * CB + k + 1)
                nc.vector.tensor_copy(by_batch(entry_next[:, :])[:, :, 1:P],
                                      by_batch(y[:, 3, :])[:, :, 0:P - 1]).then_inc(c_chain, 1)
                dve.wait_ge(c_chain, r * 2 + 1)
                nc.vector.tensor_tensor(entry_diff[:, :], entry_next[:, :], entry[:, :], ALU.subtract).then_inc(c_chain, 1)
                dve.wait_ge(c_chain, r * 2 + 2)
                nc.vector.tensor_reduce(diff_max[:, :], entry_diff[:, :], AX.X, ALU.max,
                                        apply_absolute_value=True).then_inc(diff_ready, 1)
                nc.vector.tensor_copy(entry[:, :], entry_next[:, :])
                nc.vector.tensor_copy(y[:, 3, :], entry_next[:, :]).then_inc(entry_set, 1)
                dve.wait_ge(diff_reduced, r + 1)
                nc.vector.tensor_scalar(rounds_limit[:, :], diff_all[:, :], SETTLED, float(P), ALU.is_gt,
                                        ALU.mult).then_inc(verdict, 1)
                wait_alone(dve, "dve", verdict, r + 1)
                dve.reg_load(limit, rounds_limit[0:1, 0:1])

        @block.gpsimd
        def _(pool):
            nc.gpsimd.memset(ident[:, :], 0.0).then_inc(ident_made, 1)
            nc.gpsimd.memset(zeros[:, :], 0.0)
            nc.gpsimd.memset(minus_half[:, :, :], -0.5)
            pool.wait_ge(ident_made, 1)
            nc.gpsimd.affine_select(out=ident[:, :], in_=ident[:, :], compare_op=ALU.not_equal, fill=1.0, base=0,
                                    pattern=[[-1, P]], channel_multiplier=1).then_inc(ident_made, 1)
            pool.wait_ge(ident_made, 2)
            nc.gpsimd.tensor_scalar(center[:, :], ident[:, :], -1.0 / C, None, ALU.add).then_inc(consts_done, 1)
            pool.sem_inc(a_var_read, PRIMED)
            pool.sem_inc(b_var_read, PRIMED)
            for j in range(RING):
                pool.sem_inc(x2_stored[j], 16 * PRIMED)

            def scale_quads(src, j, par, s_xs):
                for c in range(NQ):
                    nc.gpsimd.tensor_tensor(xs[:, par, c * QT:(c + 1) * QT, 0:C], quad_f(src[:, j, :], c),
                                            kv_scale[:, c * QT:(c + 1) * QT, :].to_broadcast([P, QT, C]),
                                            ALU.mult).then_inc(s_xs, 1)

            def group_a(j, par, g, first=False):
                wait_alone(pool, "pool", a_var, g + 1)
                nc.gpsimd.tensor_scalar(var_eps[:, :, 0:1], var_in[:, par, :, 0:1], 1.0 / C, LN_C_EPS, ALU.mult, ALU.add)
                nc.gpsimd.tensor_scalar(var_eps[:, :, 1:3], var_in[:, par, :, 1:3], 1.0 / C, HD_EPS * LN_C_EPS,
                                        ALU.mult, ALU.add).then_inc(a_var_read, 1)
                pool.wait_ge(a_var_read, g + 1 + PRIMED)
                nc.gpsimd.tensor_tensor(rstd[:, :, :], var_eps[:, :, :], minus_half[:, :, :], ALU.pow).then_inc(a_pool, 1)
                pool.wait_ge(a_pool, g * 2 + 1)
                if not first:
                    pool.wait_ge(a_gram, (g - 1) * NQ + PRIMED)
                nc.gpsimd.tensor_tensor(kv_scale[:, :, :], rstd[:, :, 1:2], rstd[:, :, 2:3], ALU.mult)
                nc.gpsimd.tensor_copy(r1_all[:, bass.ds(g * GT, GT)], rstd[:, :, 0])
                nc.gpsimd.tensor_copy(xs[:, par, :, C:C + 2], rstd[:, :, 1:3]).then_inc(a_pool, 1)
                pool.wait_ge(a_pool, g * 2 + 2)
                scale_quads(xg, j, par, a_xs)

            def group_b(j, par, g, first=False):
                wait_alone(pool, "pool", b_var, g + 1)
                nc.gpsimd.tensor_scalar(var_eps[:, :, 0:1], var_in[:, par, :, 0:1], 1.0 / C, LN_T_EPS, ALU.mult,
                                        ALU.add).then_inc(b_var_read, 1)
                pool.wait_ge(b_var_read, g + 1 + PRIMED)
                nc.gpsimd.tensor_tensor(rstd[:, :, 0:1], var_eps[:, :, 0:1], minus_half[:, :, 0:1], ALU.pow).then_inc(b_pool, 1)
                pool.wait_ge(b_pool, g * 2 + 1)
                if not first:
                    pool.wait_ge(b_gram, (g - 1) * NQ + PRIMED)
                nc.gpsimd.tensor_tensor(kv_scale[:, :, :], rstd[:, :, 0:1], rstd[:, :, 0:1], ALU.mult)
                nc.gpsimd.tensor_copy(r2_flat[:, bass.ds(g * GT, GT)], rstd[:, :, 0])
                nc.gpsimd.tensor_copy(xs[:, par, :, C:C + 1], rstd[:, :, 0:1]).then_inc(b_pool, 1)
                pool.wait_ge(b_pool, g * 2 + 2)
                scale_quads(x2g, j, par, b_xs)

            for group in (group_a, group_b):
                group(0, 0, 0, first=True)
                with pool.Fori(0, B * BODIES) as n:
                    g0 = pool.snap(n * RING)
                    for j in range(RING):
                        group((j + 1) % RING, (j + 1) % 2, g0 + (j + 1))

            pool.wait_ge(b_pool, 2 * (B * GB + 1))
            per_batch = r2_flat[:, 0:B * CHUNK].rearrange("p (b t) -> p b t", b=B)
            nc.gpsimd.tensor_copy(r2_all[:, :, 0:CHUNK], per_batch)
            nc.gpsimd.tensor_copy(r2_all[:, :, CHUNK:CHUNK + BT], per_batch[:, :, 0:BT]).then_inc(r2_placed, 1)
            pool.wait_ge(bn_var, 1)
            nc.gpsimd.tensor_tensor(bn_cols[:, 6:7], bn_cols[:, 5:6], minus_half[:, 0, 0:1], ALU.pow).then_inc(bn_rstd, 1)
            pool.wait_ge(r2_placed, 1)

            AHEAD = 4
            x2_half = xg[:, :, :].rearrange("p (h two) (b t c) -> p h (two b) t c", two=2, b=2, c=C)

            def normalise(s, t, token):
                half = (t // HT) % 2
                nc.gpsimd.tensor_tensor(xn[:, t % 4, :, :], x2_half[:, half, :, t % HT, :],
                                        r2_all[:, :, bass.ds(token, 1)].to_broadcast([P, B, C]), ALU.mult).then_inc(c_xn, 1)

            def body_c(n, k):
                s0 = n * BT if isinstance(n, int) else pool.snap(n * BT)
                token0 = k * BT if isinstance(k, int) else pool.snap(k * BT)
                for t in range(BT):
                    ta = t + AHEAD
                    if ta == HT:
                        pool.wait_ge(x2_in[1], n * 16 + 16)
                    if ta == BT:
                        pool.wait_ge(x2_in[0], n * 16 + 32)
                    pool.wait_ge(c_T, s0 + t + 1)
                    normalise(s0 + ta, ta, token0 + ta)

            pool.wait_ge(x2_in[0], 16)
            for t in range(AHEAD):
                normalise(t, t, (CB - 1) * BT + t)
            body_c(0, CB - 1)
            limit = pool.alloc_register("pool_limit")
            pool.reg_mov(limit, 1)
            with pool.Fori(0, limit) as r:
                with pool.Fori(0, CB) as k:
                    body_c(r * CB + k + 1, k)
                wait_alone(pool, "pool", diff_ready, r + 1)
                nc.gpsimd.partition_all_reduce(diff_all[:, :], diff_max[:, :], P,
                                               bass.bass_isa.ReduceOp.max).then_inc(diff_reduced, 1)
                wait_alone(pool, "pool", verdict, r + 1)
                pool.reg_load(limit, rounds_limit[0:1, 0:1])


_INS = ['x', 'L0_conv_Wq', 'L0_conv_Wk', 'L0_conv_Wv', 'L0_conv_gamma_k', 'L0_conv_beta_k', 'L0_ffn_W', 'L0_ffn_V',
        'L0_ffn_gamma', 'L0_ffn_beta']
_OUTS = [((4, 256, 256, 128), 'float32')]


def kernel(**inputs):
    import numpy as _np
    import concourse.bacc as _bacc
    from concourse import mybir as _mybir
    from concourse.bass_utils import run_bass_kernel_spmd as _run

    nc = _bacc.Bacc("TRN2", target_bir_lowering=False, num_devices=1)
    arrays, args = {}, []
    for name in _INS:
        a = _np.ascontiguousarray(inputs[name])
        arrays[f"in_{name}_dram"] = a
        args.append(nc.dram_tensor(f"in_{name}_dram", a.shape, _mybir.dt.from_np(a.dtype), kind="ExternalInput").ap())
    for i, (shape, dtype) in enumerate(_OUTS):
        dt = _mybir.dt.from_np(_np.dtype(dtype))
        args.append(nc.dram_tensor(f"out_{i}_dram", shape, dt, kind="ExternalOutput").ap())
    metaformer_program(nc, *args)
    r = _run(nc, [arrays], core_ids=[0])
    got = tuple(r.results[0][f"out_{i}_dram"] for i in range(len(_OUTS)))
    return got[0]
```

```python
from contextlib import ExitStack

import concourse.bass as bass
from concourse import mybir

F32 = mybir.dt.float32
F32R = mybir.dt.float32r
I32 = mybir.dt.int32
ALU = mybir.AluOpType
ACT = mybir.ActivationFunctionType
AX = mybir.AxisListType
P = 128


def metaformer_program(nc, x, Wq, Wk, Wv, gamma_k, beta_k, ffn_W, ffn_V, ffn_gamma, ffn_beta, out):
    B, HS, WS, C = x.shape
    N = HS * WS
    HEADS, HD = Wq.shape[1], Wq.shape[2]
    CHUNK = N // P
    GT = 16
    QT = 4
    NQ = GT // QT
    RING = 4
    GB = CHUNK // GT
    DQ = NQ - 1
    BODIES = GB // RING
    NCOL = B * P
    BT = 16
    HT = BT // 2
    CB = CHUNK // BT
    LN_C_EPS, HD_EPS, LN_T_EPS, BN_EPS = 1e-6, 1e-5, 1e-5, 1e-5
    SETTLED = 2.0 ** -20
    assert C == P and HEADS * HD == P and B * C == 512 and CB * BT == CHUNK

    x_g = x.rearrange("b h w c -> b (h w c)").rearrange("b (p f) -> b p f", p=P)
    out_g = out.rearrange("b h w c -> b (h w c)").rearrange("b (p f) -> p b f", p=P)
    x2_dram = nc.dram_tensor("x2_scratch", [CHUNK // HT, P, B, HT * C], F32, kind="Internal").ap()

    with ExitStack() as ctx:
        def sb(name, shape, dt=F32):
            return ctx.enter_context(nc.sbuf_tensor(name, shape, dt))

        def sem(name):
            return ctx.enter_context(nc.semaphore(name))

        xg = sb("xg", [P, RING, GT * C])
        x2g = sb("x2g", [P, RING, GT * C])
        xs = sb("xs", [P, 2, GT, C + 2])
        xT_hi = sb("xT_hi", [P, 4, QT * P], F32R)
        xT_lo = sb("xT_lo", [P, 4, QT * P], F32R)
        xT = sb("xT", [P, 4, QT * P])
        xn = sb("xn", [P, 4, B, C])
        y = sb("y", [P, 4, NCOL])
        entry = sb("entry", [P, NCOL])
        entry_next = sb("entry_next", [P, NCOL])
        entry_diff = sb("entry_diff", [P, NCOL])
        diff_max = sb("diff_max", [P, 1])
        diff_all = sb("diff_all", [P, 1])
        rounds_limit = sb("rounds_limit", [P, 1], I32)
        r1_all = sb("r1_all", [P, B * CHUNK + GT])
        r2_flat = sb("r2_flat", [P, B * CHUNK + GT])
        r2_all = sb("r2_all", [P, B, CHUNK + BT])
        r1_now = sb("r1_now", [P, 2, GT])
        x_stats = sb("x_stats", [P, 2, GT, 6])
        z_stats = sb("z_stats", [P, NQ, 2, 6])
        z_sq = sb("z_sq", [P, 2, NQ, 2, 2])
        mean_gap = sb("mean_gap", [P, GT, 1])
        sum_sq = sb("sum_sq", [P, GT, 1])
        gap_sq = sb("gap_sq", [P, GT, 1])
        var_c = sb("var_c", [P, 2, GT, 3])
        std_c = sb("std_c", [P, 2, GT, 3])
        rstd_c = sb("rstd_c", [P, 2, GT, 3])
        newton = sb("newton", [P, 3, GT, 3])
        rstd = sb("rstd", [P, GT, 3])
        kv_scale = sb("kv_scale", [P, GT, 1])
        ident = sb("ident", [P, P])
        center = sb("center", [P, P])
        zeros = sb("zeros", [P, C + 2])
        w_in = sb("w_in", [P, 5, P])
        gamma_row = sb("gamma_row", [P, P])
        beta_row = sb("beta_row", [1, P])
        bn_gamma = sb("bn_gamma", [P, 1])
        bn_beta = sb("bn_beta", [P, 1])
        w_kv = sb("w_kv", [P, 2, 2 * P])
        w_kv_hi = sb("w_kv_hi", [P, 2, 2 * P], F32R)
        w_kv_lo = sb("w_kv_lo", [P, 2, 2 * P], F32R)
        w_c = sb("w_c", [P, 3, P])
        w_mean = sb("w_mean", [P, 3])
        w_kvg = sb("w_kvg", [P, 2, P])
        w_qT = sb("w_qT", [P, P])
        f_c = sb("f_c", [P, P])
        f_cT = sb("f_cT", [P, P])
        f_scaled = sb("f_scaled", [P, P])
        f_scaledT = sb("f_scaledT", [P, P])
        f_hi = sb("f_hi", [P, P], F32R)
        f_lo = sb("f_lo", [P, P], F32R)
        v_T = sb("v_T", [P, P])
        gram = sb("gram", [P, B, C + 2])
        gram2 = sb("gram2", [P, C + 1])
        gram_v = sb("gram_v", [P, B, P])
        rows = sb("rows", [1, 2, B, P])
        kv_heads = sb("kv_heads", [P, B, P])
        m_all = sb("m_all", [P, B * P])
        bn_prod = sb("bn_prod", [P, P])
        bn_cols = sb("bn_cols", [P, 8])

        pT = ctx.enter_context(nc.psum_tensor("pT", [P, 2, 512], F32))
        pZ = ctx.enter_context(nc.psum_tensor("pZ", [P, 2, 2, 512], F32))
        pG = ctx.enter_context(nc.psum_tensor("pG", [P, 512], F32))
        pM = ctx.enter_context(nc.psum_tensor("pM", [P, 512], F32))

        w_loaded = sem("w_loaded")
        consts_done, ident_made = sem("consts_done"), sem("ident_made")
        setup_pe, setup_dve, dve_chain, setup_done = sem("setup_pe"), sem("setup_dve"), sem("dve_chain"), sem("setup_done")
        bn_var, bn_std, r2_placed = sem("bn_var"), sem("bn_std"), sem("r2_placed")
        a_lo, a_sq, a_std, a_rstd = sem("a_lo"), sem("a_sq"), sem("a_std"), sem("a_rstd")
        b_std, b_rstd, c_hi = sem("b_std"), sem("b_rstd"), sem("c_hi")
        x_in = [sem(f"x_in{j}") for j in range(RING)]
        a_T, a_xT, a_z, a_z_read = sem("a_T"), sem("a_xT"), sem("a_z"), sem("a_z_read")
        a_small, a_var, a_var_read = sem("a_small"), sem("a_var"), sem("a_var_read")
        a_pool, a_xs, a_gram, gram_saved = sem("a_pool"), sem("a_xs"), sem("a_gram"), sem("gram_saved")
        b_T, b_xT, b_u, b_x2 = sem("b_T"), sem("b_xT"), sem("b_u"), sem("b_x2")
        b_scaled, b_added = sem("b_scaled"), sem("b_added")
        b_small, b_var, b_var_read = sem("b_small"), sem("b_var"), sem("b_var_read")
        b_pool, b_xs, b_gram, b_r1 = sem("b_pool"), sem("b_xs"), sem("b_gram"), sem("b_r1")
        x2_stored = [sem(f"x2_stored{j}") for j in range(RING)]
        x2_in = [sem(f"x2_in{j}") for j in range(2)]
        out_stored = [sem(f"out_stored{j}") for j in range(2)]
        c_xn, c_T, c_xT, c_pre, c_w, c_y = sem("c_xn"), sem("c_T"), sem("c_xT"), sem("c_pre"), sem("c_w"), sem("c_y")
        c_back, c_out = sem("c_back"), sem("c_out")
        c_chain, entry_set, diff_ready, diff_reduced, verdict = (
            sem("c_chain"), sem("entry_set"), sem("diff_ready"), sem("diff_reduced"), sem("verdict"))

        PRIMED = 1

        def tile(buf, j, t):
            return buf[:, j, t * C:(t + 1) * C]

        def quad_f(ap, c):
            return ap[:, c * QT * C:(c + 1) * QT * C].rearrange("p (t c) -> p t c", c=C)

        def wait_pos(eng, s, value):
            if not (isinstance(value, int) and value <= 0):
                eng.wait_ge(s, value)

        passed = {e: sem(f"passed_{e}") for e in ("sp", "pe", "act", "dve", "pool")}

        def wait_alone(eng, who, s, value):
            eng.wait_ge(s, value)
            eng.sem_inc(passed[who], 1)

        block = ctx.enter_context(nc.Block())

        @block.sync
        def _(sp):
            def load_x(b, g, j):
                sp.dma_start(xg[:, j, :], x_g[b, :, bass.ds(g * (GT * C), GT * C)]).then_inc(x_in[j], 16)

            for n, w in enumerate((Wq, Wk, Wv)):
                sp.dma_start(w_in[:, n, :], w.rearrange("c h d -> c (h d)")).then_inc(w_loaded, 16)
            sp.dma_start(w_in[:, 3, :], ffn_W).then_inc(w_loaded, 16)
            sp.dma_start(w_in[:, 4, :], ffn_V).then_inc(w_loaded, 16)
            sp.dma_start(gamma_row[:, :], gamma_k.rearrange("h d -> (h d)").partition_broadcast(P)).then_inc(w_loaded, 16)
            sp.dma_start(beta_row[:, :], beta_k.rearrange("(a h) d -> a (h d)", a=1)).then_inc(w_loaded, 16)
            sp.dma_start(bn_gamma[:, :], ffn_gamma.rearrange("(p a) -> p a", a=1)).then_inc(w_loaded, 16)
            sp.dma_start(bn_beta[:, :], ffn_beta.rearrange("(p a) -> p a", a=1)).then_inc(w_loaded, 16)

            for j in range(RING):
                load_x(0, j, j)

            def refill_a(b, i):
                for j in range(RING):
                    wait_alone(sp, "sp", a_gram, b * (GB * NQ) + i * (RING * NQ) + (j + 1 - RING) * NQ + PRIMED)
                    load_x(b, i * RING + j, j)

            with sp.Fori(1, BODIES) as i:
                refill_a(0, i)
            with sp.Fori(1, B) as b:
                with sp.Fori(0, BODIES) as i:
                    refill_a(b, i)
            for j in range(RING):
                sp.wait_ge(a_gram, B * GB * NQ + (j + 1 - RING) * NQ + PRIMED)
                load_x(0, j, j)

            def store_x2(b, i, j):
                sp.dma_start(
                    x2_dram[bass.ds((i * RING + j) * 2, 2), :, b, :].rearrange("k p f -> p k f"),
                    x2g[:, j, :].rearrange("p (k f) -> p k f", k=2)).then_inc(x2_stored[j], 16)

            def step_b(b, i, load):
                for j in range(RING):
                    wait_alone(sp, "sp", b_gram, b * (GB * NQ) + i * (RING * NQ) + (j + 1) * NQ + PRIMED)
                    load(j)
                    store_x2(b, i, j)

            with sp.Fori(0, B - 1) as b:
                with sp.Fori(0, BODIES - 1) as i:
                    step_b(b, i, lambda j: load_x(b, (i + 1) * RING + j, j))
                step_b(b, BODIES - 1, lambda j: load_x(b + 1, j, j))
            with sp.Fori(0, BODIES - 1) as i:
                step_b(B - 1, i, lambda j: load_x(B - 1, (i + 1) * RING + j, j))
            step_b(B - 1, BODIES - 1, lambda j: load_x(0, j, j) if j < 2 else None)
            for j in range(RING):
                sp.wait_ge(x2_stored[j], 16 * (B * BODIES + PRIMED))

            def load_x2(k, half):
                sp.dma_start(xg[:, 2 * half:2 * half + 2, :].rearrange("p a f -> p (a f)"),
                             x2_dram[bass.ds(k * 2 + half, 1), :, :, :].rearrange("a p b f -> p (a b f)")
                             ).then_inc(x2_in[half], 16)

            def step_c(n, k, k_next):
                for half in range(2):
                    wait_alone(sp, "sp", c_out, n * BT + (half + 1) * HT)
                    load_x2(k_next, half)
                    sp.dma_start(out_g[:, :, bass.ds(k * (BT * C) + half * (HT * C), HT * C)],
                                 x2g[:, 2 * half:2 * half + 2, :].rearrange("p a (b f) -> p (a b) f", b=2)
                                 ).then_inc(out_stored[half], 16)

            for j in range(2):
                sp.wait_ge(x_in[j], 16 * (2 * B * BODIES + 1))
            sp.wait_ge(b_T, (B * GB + 1) * NQ + 2)
            sp.wait_ge(b_x2, (B * GB + 1) * DQ)
            sp.wait_ge(b_added, B * GB + 1)
            load_x2(CB - 1, 0)
            load_x2(CB - 1, 1)
            step_c(0, CB - 1, 0)
            limit = sp.alloc_register("sp_limit")
            sp.reg_mov(limit, 1)
            with sp.Fori(0, limit) as r:
                with sp.Fori(0, CB - 1) as k:
                    step_c(r * CB + k + 1, k, k + 1)
                step_c(r * CB + CB, CB - 1, 0)
                for half in range(2):
                    wait_alone(sp, "sp", out_stored[half], r * (16 * CB) + 16 * (CB + 1))
                    wait_alone(sp, "sp", x2_in[half], r * (16 * CB) + 16 * (CB + 2))
                wait_alone(sp, "sp", verdict, r + 1)
                sp.reg_load(limit, rounds_limit[0:1, 0:1])

        @block.tensor
        def _(pe):
            pe.wait_ge(w_loaded, 16 * 9)
            pe.wait_ge(consts_done, 1)
            for n in range(3):
                last = nc.tensor.matmul(pM[:, n * P:(n + 1) * P], center[:, :], w_in[:, n, :], start=True, stop=True)
            last.then_inc(setup_pe, 1)
            nc.tensor.transpose(pT[:, 0, 0:P], w_in[:, 4, :], ident[:, :]).then_inc(setup_pe, 1)
            pe.wait_ge(setup_dve, 1)
            nc.tensor.transpose(pT[:, 1, 0:P], w_c[:, 0, :], ident[:, :]).then_inc(setup_pe, 1)
            pe.wait_ge(setup_dve, 2)
            nc.tensor.transpose(pG[:, 0:P], f_c[:, :], ident[:, :]).then_inc(setup_pe, 1)
            pe.wait_ge(setup_done, 1)

            def transposes(src, s_T, s_xT, j, c, q, first=False, loads=None):
                if loads is not None:
                    pe.wait_ge(x_in[j], loads)
                if not first:
                    pe.wait_ge(s_xT, q - 1)
                for t in range(QT):
                    last = nc.tensor.transpose(pT[:, c % 2, t * P:(t + 1) * P], tile(src, j, c * QT + t), ident[:, :])
                last.then_inc(s_T, 1)

            def group_a(j, q0, first=False):
                for c in range(2, NQ):
                    transposes(xg, a_T, a_lo, j, c, q0 + c)
                for c in range(NQ):
                    q = q0 + c
                    pe.wait_ge(a_lo, q + 1)
                    if not (first and c < 2):
                        pe.wait_ge(a_z_read, q - 1)
                        pe.wait_ge(a_sq, q - 1)
                    for t in range(QT):
                        z = pZ[:, c % 2, t // 2, (t % 2) * 2 * P:(t % 2 + 1) * 2 * P]
                        hi, lo = (part[:, c % 4, t * P:(t + 1) * P] for part in (xT_hi, xT_lo))
                        nc.tensor.matmul(z, hi, w_kv_hi[:, t // 2, :], start=True, stop=False)
                        nc.tensor.matmul(z, hi, w_kv_lo[:, t // 2, :], start=False, stop=False)
                        last = nc.tensor.matmul(z, lo, w_kv_hi[:, t // 2, :], start=False, stop=True)
                    last.then_inc(a_z, 1)

            def gram_quad(s_xs, s_gram, src, ring, width, j, c, need):
                pe.wait_ge(s_xs, need)
                for t in range(QT):
                    last = nc.tensor.matmul(pG[:, 0:width], tile(src, j, c * QT + t),
                                            xs[:, ring, c * QT + t, 0:width], start=False, stop=False,
                                            skip_group_check=True)
                last.then_inc(s_gram, 1)

            def open_gram(width):
                return nc.tensor.matmul(pG[:, 0:width], zeros[:, 0:P], zeros[:, 0:width], start=True, stop=False,
                                        skip_group_check=True)

            transposes(xg, a_T, a_lo, 0, 0, 0, first=True, loads=16)
            transposes(xg, a_T, a_lo, 0, 1, 1, first=True)
            group_a(0, 0, first=True)
            transposes(xg, a_T, a_lo, 1, 0, NQ, loads=16)
            transposes(xg, a_T, a_lo, 1, 1, NQ + 1)
            open_gram(C + 2).then_inc(a_gram, PRIMED)
            with pe.Fori(0, B) as b:
                pe.wait_ge(gram_saved, b + PRIMED)
                open_gram(C + 2)
                with pe.Fori(0, BODIES) as i:
                    n = pe.snap(b * BODIES + i)
                    q0 = pe.snap(n * (RING * NQ))
                    for j in range(RING):
                        j1, j2 = (j + 1) % RING, (j + 2) % RING
                        group_a(j1, q0 + (j + 1) * NQ)
                        for c in range(NQ):
                            gram_quad(a_xs, a_gram, xg, j % 2, C + 2, j, c, q0 + j * NQ + c + 1)
                            if c < 2:
                                transposes(xg, a_T, a_lo, j2, c, q0 + (j + 2) * NQ + c,
                                           loads=n * 16 + 16 * (1 + (j + 2) // RING))

            pe.wait_ge(gram_saved, B + PRIMED)
            pe.wait_ge(a_lo, (B * GB + 1) * NQ + 2)
            for b in range(B):
                last = nc.tensor.matmul(pM[:, b * P:(b + 1) * P], gram[:, b, 0:C], w_kvg[:, 1, :], start=True, stop=True)
            last.then_inc(setup_pe, 1)
            for n in range(2):
                for b in range(B):
                    last = nc.tensor.matmul(pT[0:1, n, b * P:(b + 1) * P], gram[:, b, C + n:C + n + 1],
                                            w_kvg[:, n, :], start=True, stop=True)
            last.then_inc(setup_pe, 1)
            pe.wait_ge(setup_dve, 3)
            nc.tensor.matmul(pZ[:, 0, 0, :], w_kvg[:, 0, :], gram_v[:, :, :].rearrange("p b c -> p (b c)"),
                             start=True, stop=False, skip_group_check=True)
            for b in range(B):
                nc.tensor.matmul(pZ[:, 0, 0, b * P:(b + 1) * P], rows[0:1, 0, b, :], beta_row[:, :],
                                 start=False, stop=False, skip_group_check=True)
            nc.tensor.matmul(pZ[:, 0, 0, :], beta_row[:, :], rows[0:1, 1, :, :].rearrange("a b c -> a (b c)"),
                             start=False, stop=True, skip_group_check=True).then_inc(setup_pe, 1)
            pe.wait_ge(setup_dve, 4)
            nc.tensor.matmul(pM[:, :], w_qT[:, :], kv_heads[:, :, :].rearrange("p b c -> p (b c)"),
                             start=True, stop=True).then_inc(setup_pe, 1)
            pe.wait_ge(setup_dve, 5)

            def group_b(j, g, q0, m_now, first=False):
                for c in range(2, NQ):
                    transposes(xg, b_T, b_xT, j, c, q0 + c)
                for c in range(NQ):
                    q = q0 + c
                    pe.wait_ge(b_xT, q + 1)
                    if c == DQ and not first:
                        pe.wait_ge(b_scaled, g)
                    elif not first:
                        pe.wait_ge(b_x2, (g - 1) * DQ + c + 1)
                    for t in range(QT):
                        last = nc.tensor.matmul(pZ[:, c % 2, c // 2, t * P:(t + 1) * P],
                                                xT[:, c % 4, t * P:(t + 1) * P], m_now, start=True, stop=True)
                    last.then_inc(b_u, 1)

            A_LOADS = 16 * B * BODIES
            transposes(xg, b_T, b_xT, 0, 0, 0, first=True, loads=A_LOADS + 16)
            transposes(xg, b_T, b_xT, 0, 1, 1, first=True)
            group_b(0, 0, 0, m_all[:, 0:P], first=True)
            transposes(xg, b_T, b_xT, 1, 0, NQ, loads=A_LOADS + 16)
            transposes(xg, b_T, b_xT, 1, 1, NQ + 1)
            open_gram(C + 1).then_inc(b_gram, PRIMED)
            with pe.Fori(0, B) as b:
                def body_b(i, b_next):
                    n = pe.snap(b * BODIES + i)
                    q0 = pe.snap(n * (RING * NQ))
                    g0 = pe.snap(n * RING)
                    for j in range(RING):
                        j1, j2 = (j + 1) % RING, (j + 2) % RING
                        bb = b if j < RING - 1 else b_next
                        group_b(j1, g0 + (j + 1), q0 + (j + 1) * NQ, m_all[:, bass.ds(bb * P, P)])
                        for c in range(NQ):
                            if c < 2:
                                transposes(xg, b_T, b_xT, j2, c, q0 + (j + 2) * NQ + c,
                                           loads=n * 16 + A_LOADS + 16 * (1 + (j + 2) // RING))
                            gram_quad(b_xs, b_gram, x2g, j % 2, C + 1, j, c, q0 + j * NQ + c + 1)

                with pe.Fori(0, BODIES - 1) as i:
                    body_b(i, b)
                body_b(BODIES - 1, pe.snap((b + 1) % B))

            pe.wait_ge(gram_saved, B + 1 + PRIMED)
            nc.tensor.matmul(pM[:, 0:P], f_cT[:, :], gram2[:, 0:C], start=True, stop=True)
            nc.tensor.matmul(pM[:, P:P + 1], f_cT[:, :], gram2[:, C:C + 1], start=True, stop=True).then_inc(setup_pe, 1)
            pe.wait_ge(setup_dve, 6)
            nc.tensor.transpose(pM[:, 0:P], f_scaled[:, :], ident[:, :]).then_inc(setup_pe, 1)
            pe.wait_ge(setup_dve, 7)
            pe.wait_ge(b_xT, (B * GB + 1) * NQ + 2)

            def forward(s, ring):
                pe.wait_ge(c_xn, s + 1)
                wait_pos(pe, c_xT, s - 1)
                for b in range(B):
                    last = nc.tensor.transpose(pT[:, ring % 2, b * P:(b + 1) * P], xn[:, ring % 4, b, :], ident[:, :])
                last.then_inc(c_T, 1)

            def project(s, ring):
                pe.wait_ge(c_xT, s + 1)
                pre = pZ[:, 0, ring % 2, :]
                nc.tensor.matmul(pre, f_hi[:, :], xT_hi[:, ring % 2, :], start=True, stop=False, skip_group_check=True)
                nc.tensor.matmul(pre, f_lo[:, :], xT_hi[:, ring % 2, :], start=False, stop=False, skip_group_check=True)
                nc.tensor.matmul(pre, f_hi[:, :], xT_lo[:, ring % 2, :], start=False, stop=False,
                                 skip_group_check=True).then_inc(c_w, 1)

            def recur(s, ring):
                nc.tensor.matmul(pZ[:, 0, ring % 2, :], v_T[:, :], y[:, (ring + 3) % 4, :], start=False, stop=True,
                                 skip_group_check=True).then_inc(c_pre, 1)

            def back(s, ring):
                pe.wait_ge(c_y, s + 1)
                wait_pos(pe, c_out, s - 1)
                for b in range(B):
                    last = nc.tensor.transpose(pZ[:, 1, ring % 2, b * P:(b + 1) * P], y[:, ring % 4, b * P:(b + 1) * P],
                                               ident[:, :])
                last.then_inc(c_back, 1)

            def body_c(n, enter):
                s0 = n * BT if isinstance(n, int) else pe.snap(n * BT)
                for t in range(BT):
                    if t or not enter:
                        pe.wait_ge(c_y, s0 + t)
                    recur(s0 + t, t)
                    forward(s0 + t + 2, t + 2)
                    project(s0 + t + 1, t + 1)
                    back(s0 + t, t)

            forward(0, 0)
            forward(1, 1)
            project(0, 0)
            pe.wait_ge(entry_set, 1)
            body_c(0, True)
            limit = pe.alloc_register("pe_limit")
            pe.reg_mov(limit, 1)
            with pe.Fori(0, limit) as r:
                wait_alone(pe, "pe", entry_set, r + 2)
                with pe.Fori(0, CB) as k:
                    body_c(r * CB + k + 1, False)
                wait_alone(pe, "pe", verdict, r + 1)
                pe.reg_load(limit, rounds_limit[0:1, 0:1])

        @block.scalar
        def _(act):
            def copy_quad(dst, s_T, s_z, s_xT, q, c, first=False):
                act.wait_ge(s_T, q + 1)
                if not first:
                    act.wait_ge(s_z, q - 3)
                nc.scalar.activation(dst[:, c % 4, :], pT[:, c % 2, :], ACT.Copy).then_inc(s_xT, 1)

            def roots(s_var, s_std, par, g, width):
                act.wait_ge(s_var, g + 1)
                nc.scalar.activation(std_c[:, par, :, 0:width], var_c[:, par, :, 0:width], ACT.Sqrt).then_inc(s_std, 1)

            def squares(q, c, par, first=False):
                act.wait_ge(a_z, q + 1)
                for t in range(2):
                    for kv in range(2):
                        z = pZ[:, c % 2, 1, (2 * t + kv) * P:(2 * t + kv + 1) * P]
                        last = nc.scalar.activation(z, z, ACT.Square, accum_out=z_sq[:, par, c, t, kv:kv + 1])
                last.then_inc(a_sq, 1)

            def group_a(q0, g, par, first=False):
                for c in range(2, NQ):
                    copy_quad(xT_hi, a_T, a_z, a_xT, q0 + c, c, first=first)
                for c in range(NQ):
                    squares(q0 + c, c, par)
                for c in range(2):
                    copy_quad(xT_hi, a_T, a_z, a_xT, q0 + NQ + c, c)
                roots(a_var, a_std, par, g, 3)

            for q in range(2):
                copy_quad(xT_hi, a_T, a_z, a_xT, q, q, first=True)
            group_a(0, 0, 0, first=True)
            with act.Fori(0, B) as b:
                with act.Fori(0, BODIES) as i:
                    n = act.snap(b * BODIES + i)
                    q0 = act.snap(n * (RING * NQ))
                    g0 = act.snap(n * RING)
                    for j in range(RING):
                        group_a(q0 + (j + 1) * NQ, g0 + (j + 1), (j + 1) % 2)
                act.wait_ge(a_gram, b * (GB * NQ) + GB * NQ + PRIMED)
                nc.scalar.activation(gram[:, bass.ds(b, 1), :].rearrange("p a c -> p (a c)"), pG[:, 0:C + 2],
                                     ACT.Copy).then_inc(gram_saved, 1)

            act.wait_ge(setup_dve, 5)

            def group_b(j, q0, g, par, stores, first=False):
                if not first:
                    roots(b_var, b_std, 1 - par, g - 1, 1)
                copy_quad(xT, b_T, b_u, b_xT, q0 + 2, 2, first=first)
                copy_quad(xT, b_T, b_u, b_xT, q0 + 3, 3, first=first)
                act.wait_ge(x2_stored[j], stores)
                act.wait_ge(b_r1, g + 1)
                act.wait_ge(b_u, q0 + NQ)
                for tt in range(DQ * QT, NQ * QT):
                    last = nc.scalar.activation(tile(x2g, j, tt), pZ[:, DQ % 2, DQ // 2, (tt % QT) * P:(tt % QT + 1) * P],
                                                ACT.Copy, scale=r1_now[:, par, tt:tt + 1])
                last.then_inc(b_scaled, 1)
                for c in range(2):
                    copy_quad(xT, b_T, b_u, b_xT, q0 + NQ + c, c)

            for q in range(2):
                copy_quad(xT, b_T, b_u, b_xT, q, q, first=True)
            group_b(0, 0, 0, 0, 16 * PRIMED, first=True)
            with act.Fori(0, B * BODIES) as n:
                q0 = act.snap(n * (RING * NQ))
                g0 = act.snap(n * RING)
                for j in range(RING):
                    group_b((j + 1) % RING, q0 + (j + 1) * NQ, g0 + (j + 1), (j + 1) % 2,
                            n * 16 + 16 * ((j + 1) // RING + PRIMED))
            act.wait_ge(b_gram, B * GB * NQ + PRIMED)
            nc.scalar.activation(gram2[:, :], pG[:, 0:C + 1], ACT.Copy).then_inc(gram_saved, 1)

            act.wait_ge(bn_var, 1)
            nc.scalar.activation(bn_cols[:, 6:7], bn_cols[:, 5:6], ACT.Sqrt).then_inc(bn_std, 1)

            def take_forward(s, ring):
                act.wait_ge(c_T, s + 1)
                wait_pos(act, c_w, s - 1)
                nc.scalar.activation(xT_hi[:, ring % 2, :], pT[:, ring % 2, :], ACT.Copy).then_inc(c_hi, 1)

            def body_c(n):
                s0 = n * BT if isinstance(n, int) else act.snap(n * BT)
                for t in range(BT):
                    act.wait_ge(c_pre, s0 + t + 1)
                    nc.scalar.activation(y[:, t % 4, :], pZ[:, 0, t % 2, :], ACT.Sigmoid,
                                         bias=bn_cols[:, 7:8]).then_inc(c_y, 1)
                    take_forward(s0 + t + 2, t + 2)

            act.wait_ge(setup_dve, 7)
            take_forward(0, 0)
            take_forward(1, 1)
            body_c(0)
            limit = act.alloc_register("act_limit")
            act.reg_mov(limit, 1)
            with act.Fori(0, limit) as r:
                with act.Fori(0, CB) as k:
                    body_c(r * CB + k + 1)
                wait_alone(act, "act", verdict, r + 1)
                act.reg_load(limit, rounds_limit[0:1, 0:1])

        @block.vector
        def _(dve):
            chain = [0]

            def link(ins):
                chain[0] += 1
                ins.then_inc(dve_chain, 1)
                dve.wait_ge(dve_chain, chain[0])

            dve.wait_ge(w_loaded, 16 * 9)
            dve.wait_ge(consts_done, 1)
            dve.wait_ge(setup_pe, 1)
            nc.vector.tensor_copy(w_kv[:, 0, 0:2 * P:2], pM[:, P:2 * P])
            nc.vector.tensor_copy(w_kv[:, 0, 1:2 * P:2], pM[:, 2 * P:3 * P])
            nc.vector.tensor_copy(w_c[:, :, :].rearrange("p a b -> p (a b)"), pM[:, 0:3 * P]).then_inc(setup_dve, 1)
            dve.wait_ge(setup_dve, 1)
            link(nc.vector.tensor_reduce(w_mean[:, :], w_c[:, :, :], AX.X, ALU.add))
            link(nc.vector.tensor_scalar(w_mean[:, :], w_mean[:, :], 1.0 / P, None, ALU.mult))
            for n in range(2):
                nc.vector.scalar_tensor_tensor(w_kvg[:, n, :], w_c[:, 1 + n, :], w_mean[:, 1 + n:2 + n], gamma_row[:, :],
                                               ALU.subtract, ALU.mult)
                nc.vector.tensor_scalar(w_kv[:, 1, n * P:(n + 1) * P], w_c[:, 1 + n, :], w_mean[:, 1 + n:2 + n], None,
                                        ALU.subtract)
            link(nc.vector.tensor_reduce(bn_cols[:, 0:1], w_in[:, 3, :], AX.X, ALU.add))
            link(nc.vector.tensor_copy(w_kv_hi[:, :, :], w_kv[:, :, :]))
            nc.vector.tensor_tensor(w_kv_lo[:, :, :], w_kv[:, :, :], w_kv_hi[:, :, :].bitcast(F32), ALU.subtract)
            link(nc.vector.tensor_scalar(bn_cols[:, 1:2], bn_cols[:, 0:1], 1.0 / P, None, ALU.mult))
            nc.vector.tensor_scalar(f_c[:, :], w_in[:, 3, :], bn_cols[:, 1:2], None, ALU.subtract).then_inc(setup_dve, 1)
            dve.wait_ge(setup_pe, 3)
            nc.vector.tensor_copy(v_T[:, :], pT[:, 0, 0:P])
            nc.vector.tensor_copy(w_qT[:, :], pT[:, 1, 0:P])
            dve.wait_ge(setup_pe, 4)
            nc.vector.tensor_copy(f_cT[:, :], pG[:, 0:P]).then_inc(setup_done, 1)
            nc.vector.memset(kv_heads[:, :, :], 0.0)
            nc.vector.memset(entry_next[:, :], 0.0)
            nc.vector.memset(y[:, 3, :], 0.0).then_inc(entry_set, 1)
            nc.vector.memset(entry[:, :], 0.0).then_inc(gram_saved, PRIMED)

            def var_of_x(s_small, par, base, eps):
                dve.wait_ge(s_small, base + 1)
                nc.vector.tensor_tensor(mean_gap[:, :, :], x_stats[:, par, :, 1:2], x_stats[:, par, :, 4:5], ALU.subtract)
                nc.vector.scalar_tensor_tensor(sum_sq[:, :, :], x_stats[:, par, :, 2:3], C * eps, x_stats[:, par, :, 5:6],
                                               ALU.add, ALU.add).then_inc(s_small, 1)
                dve.wait_ge(s_small, base + 2)
                nc.vector.scalar_tensor_tensor(gap_sq[:, :, :], mean_gap[:, :, :], C / 4.0, mean_gap[:, :, :],
                                               ALU.mult, ALU.mult).then_inc(s_small, 1)
                dve.wait_ge(s_small, base + 3)
                return nc.vector.tensor_tensor(var_c[:, par, :, 0:1], sum_sq[:, :, :], gap_sq[:, :, :], ALU.add)

            def reciprocals(s_std, s_rstd, par, g, width):
                dve.wait_ge(s_std, g + 1)
                nc.vector.reciprocal(rstd_c[:, par, :, 0:width], std_c[:, par, :, 0:width]).then_inc(s_rstd, 1)

            by_quad = lambda ap: ap.rearrange("p (c t) w -> p c t w", c=NQ)

            def take_low(q, c, first=False):
                dve.wait_ge(a_xT, q + 1)
                if not first:
                    dve.wait_ge(a_z, q - 3)
                nc.vector.tensor_tensor(xT_lo[:, c % 4, :], pT[:, c % 2, :], xT_hi[:, c % 4, :].bitcast(F32),
                                        ALU.subtract).then_inc(a_lo, 1)

            def stats_of_x(j, par, first_tile, count):
                for t in range(first_tile, first_tile + count):
                    last = nc.vector.bn_stats(x_stats[:, par, t, :], tile(xg, j, t))
                return last

            def group_a(j, par, q0, g, loads, first=False):
                j_next = (j + 1) % RING

                def stats_of_z(c):
                    dve.wait_ge(a_z, q0 + c + 1)
                    for t in range(2):
                        last = nc.vector.bn_stats(z_stats[:, c, t, :], pZ[:, c % 2, 0, t * 2 * P:(t + 1) * 2 * P])
                    last.then_inc(a_z_read, 1)

                if not first:
                    dve.wait_ge(a_var, g)
                dve.wait_ge(x_in[j_next], loads)
                stats_of_x(j_next, 1 - par, 0, 2)
                take_low(q0 + 2, 2, first=first)
                if not first:
                    reciprocals(a_std, a_rstd, 1 - par, g - 1, 3)
                stats_of_z(0)
                take_low(q0 + 3, 3, first=first)
                stats_of_x(j_next, 1 - par, 2, 2)
                stats_of_z(1)
                stats_of_x(j_next, 1 - par, 4, 1)
                stats_of_z(2)
                stats_of_x(j_next, 1 - par, 5, 3)
                stats_of_z(3)
                stats_of_x(j_next, 1 - par, 8, 1)
                if not first:
                    dve.wait_ge(a_var_read, g - 2 + 1 + PRIMED)
                var_of_x(a_small, par, g * 4, LN_C_EPS).then_inc(a_small, 1)
                dve.wait_ge(a_small, g * 4 + 4)
                dve.wait_ge(a_z_read, q0 + NQ)
                dve.wait_ge(a_sq, q0 + NQ)
                var_q = by_quad(var_c[:, par, :, :])
                for kv in range(2):
                    for pair, m2 in ((slice(0, 2), z_stats[:, :, :, 2 + 3 * kv]), (slice(2, 4), z_sq[:, par, :, :, kv])):
                        last = nc.vector.scalar_tensor_tensor(var_q[:, :, pair, 1 + kv], var_q[:, :, pair, 0], HD_EPS, m2,
                                                              ALU.mult, ALU.add)
                last.then_inc(a_var, 1)
                take_low(q0 + NQ, 0)
                stats_of_x(j_next, 1 - par, 9, 3)
                take_low(q0 + NQ + 1, 1)
                stats_of_x(j_next, 1 - par, 12, 4).then_inc(a_small, 1)

            dve.wait_ge(x_in[0], 16)
            stats_of_x(0, 0, 0, GT).then_inc(a_small, 1)
            take_low(0, 0, first=True)
            take_low(1, 1, first=True)
            group_a(0, 0, 0, 0, 16, first=True)
            with dve.Fori(0, B * BODIES) as n:
                q0 = dve.snap(n * (RING * NQ))
                g0 = dve.snap(n * RING)
                for j in range(RING):
                    group_a((j + 1) % RING, (j + 1) % 2, q0 + (j + 1) * NQ, g0 + (j + 1), n * 16 + 16 * (1 + (j + 2) // RING))
            reciprocals(a_std, a_rstd, 0, B * GB, 3)

            dve.wait_ge(setup_pe, 5)
            nc.vector.tensor_copy(gram_v[:, :, :].rearrange("p b c -> p (b c)"), pM[:, :])
            dve.wait_ge(setup_pe, 6)
            nc.vector.scalar_tensor_tensor(rows[:, 0, :, :], beta_row[:, :].unsqueeze(1).to_broadcast([1, B, P]), float(N),
                                           pT[0:1, 0, :].rearrange("a (b c) -> a b c", b=B), ALU.mult, ALU.add)
            nc.vector.tensor_copy(rows[:, 1, :, :], pT[0:1, 1, :].rearrange("a (b c) -> a b c", b=B)).then_inc(setup_dve, 1)
            dve.wait_ge(setup_pe, 7)
            for h in range(HEADS):
                hs = slice(h * HD, (h + 1) * HD)
                last = nc.vector.tensor_scalar(kv_heads[hs, :, hs],
                                               pZ[:, 0, 0, :].rearrange("p (b c) -> p b c", b=B)[hs, :, hs],
                                               1.0 / N, None, ALU.mult)
            last.then_inc(setup_dve, 1)
            dve.wait_ge(setup_pe, 8)
            nc.vector.tensor_copy(m_all[:, :].rearrange("p (b e h) -> p b h e", b=B, h=HEADS),
                                  pM[:, :].rearrange("p (b h e) -> p b h e", b=B, h=HEADS)).then_inc(setup_dve, 1)

            def group_b(j, par, q0, g, loads, stores, first=False):
                if not first:
                    reciprocals(b_std, b_rstd, 1 - par, g - 1, 1)
                nc.vector.tensor_copy(r1_now[:, par, :], r1_all[:, bass.ds(g * GT, GT)]).then_inc(b_r1, 1)
                dve.wait_ge(b_r1, g + 1)
                dve.wait_ge(x_in[j], loads)
                dve.wait_ge(x2_stored[j], stores)
                if not first:
                    dve.wait_ge(b_var, g)

                def stats(c):
                    if c < DQ:
                        dve.wait_ge(b_x2, g * DQ + c + 1)
                    else:
                        dve.wait_ge(b_added, g + 1)
                    for t in range(QT):
                        last = nc.vector.bn_stats(x_stats[:, par, c * QT + t, :], tile(x2g, j, c * QT + t))
                    return last

                for c in range(DQ):
                    dve.wait_ge(b_u, q0 + c + 1)
                    for t in range(QT):
                        tt = c * QT + t
                        last = nc.vector.scalar_tensor_tensor(
                            tile(x2g, j, tt), pZ[:, c % 2, c // 2, t * P:(t + 1) * P], r1_now[:, par, tt:tt + 1],
                            tile(xg, j, tt), ALU.mult, ALU.add)
                    last.then_inc(b_x2, 1)
                    if c:
                        stats(c - 1)
                stats(DQ - 1)
                stats(NQ - 1).then_inc(b_small, 1)
                if not first:
                    dve.wait_ge(b_var_read, g - 2 + 1 + PRIMED)
                var_of_x(b_small, par, g * 3, LN_T_EPS).then_inc(b_var, 1)

            A_LOADS = 16 * B * BODIES
            dve.wait_ge(a_xs, (B * GB + 1) * NQ)
            group_b(0, 0, 0, 0, A_LOADS + 16, 16 * PRIMED, first=True)
            with dve.Fori(0, B * BODIES) as n:
                q0 = dve.snap(n * (RING * NQ))
                g0 = dve.snap(n * RING)
                for j in range(RING):
                    body = (j + 1) // RING
                    group_b((j + 1) % RING, (j + 1) % 2, q0 + (j + 1) * NQ, g0 + (j + 1),
                            n * 16 + A_LOADS + 16 * (1 + body), n * 16 + 16 * (body + PRIMED))

            dve.wait_ge(setup_pe, 9)
            link(nc.vector.tensor_tensor(bn_prod[:, :], pM[:, 0:P], f_c[:, :], ALU.mult))
            nc.vector.tensor_scalar(bn_cols[:, 3:4], pM[:, P:P + 1], 1.0 / (B * N), None, ALU.mult)
            link(nc.vector.tensor_reduce(bn_cols[:, 2:3], bn_prod[:, :], AX.X, ALU.add))
            link(nc.vector.tensor_tensor(bn_cols[:, 4:5], bn_cols[:, 3:4], bn_cols[:, 3:4], ALU.mult))
            link(nc.vector.scalar_tensor_tensor(bn_cols[:, 5:6], bn_cols[:, 2:3], 1.0 / (B * N), bn_cols[:, 4:5],
                                                ALU.mult, ALU.subtract))
            nc.vector.tensor_scalar(bn_cols[:, 5:6], bn_cols[:, 5:6], BN_EPS, None, ALU.add).then_inc(bn_var, 1)
            dve.wait_ge(bn_std, 1)
            link(nc.vector.reciprocal(bn_cols[:, 0:1], bn_cols[:, 6:7]))
            link(nc.vector.tensor_tensor(bn_cols[:, 1:2], bn_cols[:, 0:1], bn_cols[:, 0:1], ALU.mult))
            link(nc.vector.tensor_tensor(bn_cols[:, 2:3], bn_cols[:, 1:2], bn_cols[:, 5:6], ALU.mult))
            link(nc.vector.tensor_scalar(bn_cols[:, 4:5], bn_cols[:, 2:3], -0.5, 1.5, ALU.mult, ALU.add))
            link(nc.vector.tensor_tensor(bn_cols[:, 6:7], bn_cols[:, 0:1], bn_cols[:, 4:5], ALU.mult))
            link(nc.vector.tensor_tensor(bn_cols[:, 0:1], bn_cols[:, 6:7], bn_gamma[:, :], ALU.mult))
            link(nc.vector.tensor_tensor(bn_cols[:, 1:2], bn_cols[:, 3:4], bn_cols[:, 0:1], ALU.mult))
            nc.vector.tensor_tensor(bn_cols[:, 7:8], bn_beta[:, :], bn_cols[:, 1:2], ALU.subtract)
            nc.vector.tensor_scalar(f_scaled[:, :], f_c[:, :], bn_cols[:, 0:1], None, ALU.mult).then_inc(setup_dve, 1)
            dve.wait_ge(setup_pe, 10)
            link(nc.vector.tensor_copy(f_scaledT[:, :], pM[:, 0:P]))
            link(nc.vector.tensor_copy(f_hi[:, :], f_scaledT[:, :]))
            nc.vector.tensor_tensor(f_lo[:, :], f_scaledT[:, :], f_hi[:, :].bitcast(F32), ALU.subtract).then_inc(setup_dve, 1)

            x2_half = xg[:, :, :].rearrange("p (h two) (b t c) -> p h (two b) t c", two=2, b=2, c=C)
            out_half = x2g[:, :, :].rearrange("p (h two) (b t c) -> p h (two b) t c", two=2, b=2, c=C)

            def take_forward(s, ring):
                dve.wait_ge(c_hi, s + 1)
                nc.vector.tensor_tensor(xT_lo[:, ring % 2, :], pT[:, ring % 2, :], xT_hi[:, ring % 2, :].bitcast(F32),
                                        ALU.subtract).then_inc(c_xT, 1)

            def body_c(n):
                s0 = n * BT if isinstance(n, int) else dve.snap(n * BT)
                for t in range(BT):
                    half = t // HT
                    take_forward(s0 + t + 2, t + 2)
                    if t % HT == 0:
                        wait_pos(dve, out_stored[half], n * 16)
                    dve.wait_ge(c_back, s0 + t + 1)
                    nc.vector.tensor_tensor(out_half[:, half, :, t % HT, :],
                                            pZ[:, 1, t % 2, :].rearrange("p (b c) -> p b c", b=B),
                                            x2_half[:, half, :, t % HT, :], ALU.add).then_inc(c_out, 1)

            by_batch = lambda ap: ap.rearrange("p (b c) -> p b c", b=B)

            dve.wait_ge(b_xs, B * GB * NQ)
            take_forward(0, 0)
            take_forward(1, 1)
            body_c(0)
            link(nc.vector.tensor_copy(by_batch(entry_next[:, :])[:, :, 1:P], by_batch(y[:, 3, :])[:, :, 0:P - 1]))
            nc.vector.tensor_copy(entry[:, :], entry_next[:, :])
            nc.vector.tensor_copy(y[:, 3, :], entry_next[:, :]).then_inc(entry_set, 1)
            limit = dve.alloc_register("dve_limit")
            dve.reg_mov(limit, 1)
            with dve.Fori(0, limit) as r:
                with dve.Fori(0, CB) as k:
                    body_c(r * CB + k + 1)
                nc.vector.tensor_copy(by_batch(entry_next[:, :])[:, :, 1:P],
                                      by_batch(y[:, 3, :])[:, :, 0:P - 1]).then_inc(c_chain, 1)
                dve.wait_ge(c_chain, r * 2 + 1)
                nc.vector.tensor_tensor(entry_diff[:, :], entry_next[:, :], entry[:, :], ALU.subtract).then_inc(c_chain, 1)
                dve.wait_ge(c_chain, r * 2 + 2)
                nc.vector.tensor_reduce(diff_max[:, :], entry_diff[:, :], AX.X, ALU.max,
                                        apply_absolute_value=True).then_inc(diff_ready, 1)
                nc.vector.tensor_copy(entry[:, :], entry_next[:, :])
                nc.vector.tensor_copy(y[:, 3, :], entry_next[:, :]).then_inc(entry_set, 1)
                dve.wait_ge(diff_reduced, r + 1)
                nc.vector.tensor_scalar(rounds_limit[:, :], diff_all[:, :], SETTLED, float(P), ALU.is_gt,
                                        ALU.mult).then_inc(verdict, 1)
                wait_alone(dve, "dve", verdict, r + 1)
                dve.reg_load(limit, rounds_limit[0:1, 0:1])

        @block.gpsimd
        def _(pool):
            nc.gpsimd.memset(ident[:, :], 0.0).then_inc(ident_made, 1)
            nc.gpsimd.memset(zeros[:, :], 0.0)
            pool.wait_ge(ident_made, 1)
            nc.gpsimd.affine_select(out=ident[:, :], in_=ident[:, :], compare_op=ALU.not_equal, fill=1.0, base=0,
                                    pattern=[[-1, P]], channel_multiplier=1).then_inc(ident_made, 1)
            pool.wait_ge(ident_made, 2)
            nc.gpsimd.tensor_scalar(center[:, :], ident[:, :], -1.0 / C, None, ALU.add).then_inc(consts_done, 1)
            pool.sem_inc(a_var_read, PRIMED)
            pool.sem_inc(b_var_read, PRIMED)
            for j in range(RING):
                pool.sem_inc(x2_stored[j], 16 * PRIMED)

            def scale_quads(src, j, par, s_xs, c0=0, c1=NQ):
                for c in range(c0, c1):
                    nc.gpsimd.tensor_tensor(xs[:, par, c * QT:(c + 1) * QT, 0:C], quad_f(src[:, j, :], c),
                                            kv_scale[:, c * QT:(c + 1) * QT, :].to_broadcast([P, QT, C]),
                                            ALU.mult).then_inc(s_xs, 1)

            ROOT_C = float(C) ** 0.5

            def refine(s_rstd, s_pool, s_read, par, g, width):
                r, v = rstd_c[:, par, :, 0:width], var_c[:, par, :, 0:width]
                r2, vr2, factor = (newton[:, i, :, 0:width] for i in range(3))
                pool.wait_ge(s_rstd, g + 1)
                nc.gpsimd.tensor_tensor(r2, r, r, ALU.mult).then_inc(s_pool, 1)
                pool.wait_ge(s_pool, g * 5 + 1)
                nc.gpsimd.tensor_tensor(vr2, r2, v, ALU.mult).then_inc(s_pool, 1)
                wait_alone(pool, "pool", s_pool, g * 5 + 2)
                nc.gpsimd.tensor_scalar(factor, vr2, -0.5 * ROOT_C, 1.5 * ROOT_C, ALU.mult, ALU.add).then_inc(s_pool, 1)
                pool.wait_ge(s_pool, g * 5 + 3)
                nc.gpsimd.tensor_tensor(rstd[:, :, 0:width], r, factor, ALU.mult).then_inc(s_pool, 1)
                wait_alone(pool, "pool", s_pool, g * 5 + 4)
                pool.sem_inc(s_read, 1)

            def group_a(j, par, g, first=False):
                refine(a_rstd, a_pool, a_var_read, par, g, 3)
                if not first:
                    pool.wait_ge(a_gram, (g - 1) * NQ + PRIMED)
                nc.gpsimd.tensor_tensor(kv_scale[:, :, :], rstd[:, :, 1:2], rstd[:, :, 2:3], ALU.mult)
                nc.gpsimd.tensor_copy(r1_all[:, bass.ds(g * GT, GT)], rstd[:, :, 0])
                nc.gpsimd.tensor_copy(xs[:, par, :, C:C + 2], rstd[:, :, 1:3]).then_inc(a_pool, 1)
                pool.wait_ge(a_pool, g * 5 + 5)
                scale_quads(xg, j, par, a_xs)

            def add_x(j, g):
                pool.wait_ge(b_scaled, g + 1)
                nc.gpsimd.tensor_tensor(quad_f(x2g[:, j, :], DQ), quad_f(x2g[:, j, :], DQ), quad_f(xg[:, j, :], DQ),
                                        ALU.add).then_inc(b_added, 1)

            def group_b(j, par, g):
                refine(b_rstd, b_pool, b_var_read, par, g, 1)
                if not (isinstance(g, int) and g == 0):
                    pool.wait_ge(b_gram, (g - 1) * NQ + PRIMED)
                nc.gpsimd.tensor_tensor(kv_scale[:, :, :], rstd[:, :, 0:1], rstd[:, :, 0:1], ALU.mult)
                nc.gpsimd.tensor_copy(r2_flat[:, bass.ds(g * GT, GT)], rstd[:, :, 0])
                nc.gpsimd.tensor_copy(xs[:, par, :, C:C + 1], rstd[:, :, 0:1]).then_inc(b_pool, 1)
                pool.wait_ge(b_pool, g * 5 + 5)
                scale_quads(x2g, j, par, b_xs, 0, NQ - 1)
                add_x((j + 1) % RING, g + 1)
                scale_quads(x2g, j, par, b_xs, NQ - 1, NQ)

            group_a(0, 0, 0, first=True)
            with pool.Fori(0, B * BODIES) as n:
                g0 = pool.snap(n * RING)
                for j in range(RING):
                    group_a((j + 1) % RING, (j + 1) % 2, g0 + (j + 1))

            add_x(0, 0)
            group_b(0, 0, 0)
            with pool.Fori(0, B * BODIES - 1) as n:
                g0 = pool.snap(n * RING)
                for j in range(RING):
                    group_b((j + 1) % RING, (j + 1) % 2, g0 + (j + 1))
            for j in range(1, RING):
                group_b(j, j % 2, (B * BODIES - 1) * RING + j)

            pool.wait_ge(b_pool, 5 * B * GB)
            per_batch = r2_flat[:, 0:B * CHUNK].rearrange("p (b t) -> p b t", b=B)
            nc.gpsimd.tensor_copy(r2_all[:, :, 0:CHUNK], per_batch)
            nc.gpsimd.tensor_copy(r2_all[:, :, CHUNK:CHUNK + BT], per_batch[:, :, 0:BT]).then_inc(r2_placed, 1)
            pool.wait_ge(r2_placed, 1)

            AHEAD = 4
            x2_half = xg[:, :, :].rearrange("p (h two) (b t c) -> p h (two b) t c", two=2, b=2, c=C)

            def normalise(s, t, token):
                half = (t // HT) % 2
                nc.gpsimd.tensor_tensor(xn[:, t % 4, :, :], x2_half[:, half, :, t % HT, :],
                                        r2_all[:, :, bass.ds(token, 1)].to_broadcast([P, B, C]), ALU.mult).then_inc(c_xn, 1)

            def body_c(n, k):
                s0 = n * BT if isinstance(n, int) else pool.snap(n * BT)
                token0 = k * BT if isinstance(k, int) else pool.snap(k * BT)
                for t in range(BT):
                    ta = t + AHEAD
                    if ta == HT:
                        pool.wait_ge(x2_in[1], n * 16 + 16)
                    if ta == BT:
                        pool.wait_ge(x2_in[0], n * 16 + 32)
                    pool.wait_ge(c_T, s0 + t + 1)
                    normalise(s0 + ta, ta, token0 + ta)

            pool.wait_ge(x2_in[0], 16)
            for t in range(AHEAD):
                normalise(t, t, (CB - 1) * BT + t)
            body_c(0, CB - 1)
            limit = pool.alloc_register("pool_limit")
            pool.reg_mov(limit, 1)
            with pool.Fori(0, limit) as r:
                with pool.Fori(0, CB) as k:
                    body_c(r * CB + k + 1, k)
                wait_alone(pool, "pool", diff_ready, r + 1)
                nc.gpsimd.partition_all_reduce(diff_all[:, :], diff_max[:, :], P,
                                               bass.bass_isa.ReduceOp.max).then_inc(diff_reduced, 1)
                wait_alone(pool, "pool", verdict, r + 1)
                pool.reg_load(limit, rounds_limit[0:1, 0:1])


_INS = ['x', 'L0_conv_Wq', 'L0_conv_Wk', 'L0_conv_Wv', 'L0_conv_gamma_k', 'L0_conv_beta_k', 'L0_ffn_W', 'L0_ffn_V',
        'L0_ffn_gamma', 'L0_ffn_beta']
_OUTS = [((4, 256, 256, 128), 'float32')]


def kernel(**inputs):
    import numpy as _np
    import concourse.bacc as _bacc
    from concourse import mybir as _mybir
    from concourse.bass_utils import run_bass_kernel_spmd as _run

    nc = _bacc.Bacc("TRN2", target_bir_lowering=False, num_devices=1)
    arrays, args = {}, []
    for name in _INS:
        a = _np.ascontiguousarray(inputs[name])
        arrays[f"in_{name}_dram"] = a
        args.append(nc.dram_tensor(f"in_{name}_dram", a.shape, _mybir.dt.from_np(a.dtype), kind="ExternalInput").ap())
    for i, (shape, dtype) in enumerate(_OUTS):
        dt = _mybir.dt.from_np(_np.dtype(dtype))
        args.append(nc.dram_tensor(f"out_{i}_dram", shape, dt, kind="ExternalOutput").ap())
    metaformer_program(nc, *args)
    r = _run(nc, [arrays], core_ids=[0])
    got = tuple(r.results[0][f"out_{i}_dram"] for i in range(len(_OUTS)))
    return got[0]
```

```python
from contextlib import ExitStack

import concourse.bass as bass
from concourse import mybir

F32 = mybir.dt.float32
F32R = mybir.dt.float32r
I32 = mybir.dt.int32
ALU = mybir.AluOpType
ACT = mybir.ActivationFunctionType
AX = mybir.AxisListType
P = 128


def metaformer_program(nc, x, Wq, Wk, Wv, gamma_k, beta_k, ffn_W, ffn_V, ffn_gamma, ffn_beta, out):
    B, HS, WS, C = x.shape
    N = HS * WS
    HEADS, HD = Wq.shape[1], Wq.shape[2]
    CHUNK = N // P
    GT = 16
    QT = 4
    NQ = GT // QT
    RING = 4
    GB = CHUNK // GT
    DQ = NQ - 1
    BODIES = GB // RING
    NCOL = B * P
    BT = 16
    LT = 4
    PARTS = BT // LT
    CB = CHUNK // BT
    LN_C_EPS, HD_EPS, LN_T_EPS, BN_EPS = 1e-6, 1e-5, 1e-5, 1e-5
    SETTLED = 2.0 ** -20
    assert B * LT == GT
    assert C == P and HEADS * HD == P and B * C == 512 and CB * BT == CHUNK

    x_g = x.rearrange("b h w c -> b (h w c)").rearrange("b (p f) -> b p f", p=P)
    out_g = out.rearrange("b h w c -> b (h w c)").rearrange("b (p f) -> p b f", p=P)
    x2_dram = nc.dram_tensor("x2_scratch", [CHUNK // LT, P, B, LT * C], F32, kind="Internal").ap()

    with ExitStack() as ctx:
        def sb(name, shape, dt=F32):
            return ctx.enter_context(nc.sbuf_tensor(name, shape, dt))

        def sem(name):
            return ctx.enter_context(nc.semaphore(name))

        xg = sb("xg", [P, RING, GT * C])
        x2g = sb("x2g", [P, RING, GT * C])
        xs = sb("xs", [P, 2, GT, C + 2])
        xT_hi = sb("xT_hi", [P, 4, QT * P], F32R)
        xT_lo = sb("xT_lo", [P, 4, QT * P], F32R)
        xT = sb("xT", [P, 4, QT * P])
        xn = sb("xn", [P, 4, B, C])
        y = sb("y", [P, 4, NCOL])
        entry = sb("entry", [P, NCOL])
        entry_next = sb("entry_next", [P, NCOL])
        entry_diff = sb("entry_diff", [P, NCOL])
        diff_max = sb("diff_max", [P, 1])
        diff_all = sb("diff_all", [P, 1])
        rounds_limit = sb("rounds_limit", [P, 1], I32)
        r1_all = sb("r1_all", [P, B * CHUNK + GT])
        r2_all = sb("r2_all", [P, B * CHUNK])
        r1_now = sb("r1_now", [P, 2, GT])
        x_stats = sb("x_stats", [P, 2, GT, 6])
        z_stats = sb("z_stats", [P, NQ, 2, 6])
        z_sq = sb("z_sq", [P, 2, NQ, 2, 2])
        mean_gap = sb("mean_gap", [P, GT, 1])
        sum_sq = sb("sum_sq", [P, GT, 1])
        gap_sq = sb("gap_sq", [P, GT, 1])
        var_c = sb("var_c", [P, 2, GT, 3])
        std_c = sb("std_c", [P, 2, GT, 3])
        rstd_c = sb("rstd_c", [P, 2, GT, 3])
        newton = sb("newton", [P, 3, GT, 3])
        rstd = sb("rstd", [P, GT, 3])
        kv_scale = sb("kv_scale", [P, GT, 1])
        ident = sb("ident", [P, P])
        center = sb("center", [P, P])
        zeros = sb("zeros", [P, C + 2])
        w_in = sb("w_in", [P, 5, P])
        gamma_row = sb("gamma_row", [P, P])
        beta_row = sb("beta_row", [1, P])
        bn_gamma = sb("bn_gamma", [P, 1])
        bn_beta = sb("bn_beta", [P, 1])
        w_kv = sb("w_kv", [P, 2, 2 * P])
        w_kv_hi = sb("w_kv_hi", [P, 2, 2 * P], F32R)
        w_kv_lo = sb("w_kv_lo", [P, 2, 2 * P], F32R)
        w_c = sb("w_c", [P, 3, P])
        w_mean = sb("w_mean", [P, 3])
        w_kvg = sb("w_kvg", [P, 2, P])
        w_qT = sb("w_qT", [P, P])
        f_c = sb("f_c", [P, P])
        f_cT = sb("f_cT", [P, P])
        f_scaled = sb("f_scaled", [P, P])
        f_scaledT = sb("f_scaledT", [P, P])
        f_hi = sb("f_hi", [P, P], F32R)
        f_lo = sb("f_lo", [P, P], F32R)
        v_T = sb("v_T", [P, P])
        gram = sb("gram", [P, B, C + 2])
        gram2 = sb("gram2", [P, C + 1])
        gram_v = sb("gram_v", [P, B, P])
        rows = sb("rows", [1, 2, B, P])
        kv_heads = sb("kv_heads", [P, B, P])
        m_all = sb("m_all", [P, B * P])
        bn_prod = sb("bn_prod", [P, P])
        bn_cols = sb("bn_cols", [P, 8])

        pT = ctx.enter_context(nc.psum_tensor("pT", [P, 2, 512], F32))
        pZ = ctx.enter_context(nc.psum_tensor("pZ", [P, 2, 2, 512], F32))
        pG = ctx.enter_context(nc.psum_tensor("pG", [P, 512], F32))
        pM = ctx.enter_context(nc.psum_tensor("pM", [P, 512], F32))

        w_loaded, consts_done, ident_made = sem("w_loaded"), sem("consts_done"), sem("ident_made")
        setup_pe, setup_dve, setup_done = sem("setup_pe"), sem("setup_dve"), sem("setup_done")
        dve_chain = sem("dve_chain")
        gram_saved, bn_var, bn_std = sem("gram_saved"), sem("bn_var"), sem("bn_std")
        x_in = [sem(f"x_in{j}") for j in range(RING)]
        x2_stored = [sem(f"x2_stored{j}") for j in range(RING)]
        x2_in = [sem(f"x2_in{j}") for j in range(PARTS)]
        out_stored = [sem(f"out_stored{j}") for j in range(PARTS)]
        a_T, a_hi, a_lo, a_z, a_z_read, a_sq = sem("a_T"), sem("a_hi"), sem("a_lo"), sem("a_z"), sem("a_z_read"), sem("a_sq")
        b_T, b_xT, b_u, b_x2 = sem("b_T"), sem("b_xT"), sem("b_u"), sem("b_x2")
        b_scaled, b_added, b_r1 = sem("b_scaled"), sem("b_added"), sem("b_r1")
        a_small, a_var, a_std, a_rstd = sem("a_small"), sem("a_var"), sem("a_std"), sem("a_rstd")
        b_small, b_var, b_std, b_rstd = sem("b_small"), sem("b_var"), sem("b_std"), sem("b_rstd")
        a_pool, a_var_read, a_xs, a_gram = sem("a_pool"), sem("a_var_read"), sem("a_xs"), sem("a_gram")
        b_pool, b_var_read, b_xs, b_gram = sem("b_pool"), sem("b_var_read"), sem("b_xs"), sem("b_gram")
        c_xn, c_T, c_hi, c_lo, c_w = sem("c_xn"), sem("c_T"), sem("c_hi"), sem("c_lo"), sem("c_w")
        c_pre, c_y, c_back, c_out = sem("c_pre"), sem("c_y"), sem("c_back"), sem("c_out")
        c_chain, entry_set, diff_ready = sem("c_chain"), sem("entry_set"), sem("diff_ready")
        diff_reduced, verdict = sem("diff_reduced"), sem("verdict")

        PRIMED = 1

        def tile(buf, j, t):
            return buf[:, j, t * C:(t + 1) * C]

        def quad_f(ap, c):
            return ap[:, c * QT * C:(c + 1) * QT * C].rearrange("p (t c) -> p t c", c=C)

        def wait_pos(eng, s, value):
            if not (isinstance(value, int) and value <= 0):
                eng.wait_ge(s, value)

        passed = {e: sem(f"passed_{e}") for e in ("sp", "pe", "act", "dve", "pool")}

        def wait_alone(eng, who, s, value):
            eng.wait_ge(s, value)
            eng.sem_inc(passed[who], 1)

        block = ctx.enter_context(nc.Block())

        @block.sync
        def _(sp):
            def load_x(b, g, j):
                sp.dma_start(xg[:, j, :], x_g[b, :, bass.ds(g * (GT * C), GT * C)]).then_inc(x_in[j], 16)

            for n, w in enumerate((Wq, Wk, Wv)):
                sp.dma_start(w_in[:, n, :], w.rearrange("c h d -> c (h d)")).then_inc(w_loaded, 16)
            sp.dma_start(w_in[:, 3, :], ffn_W).then_inc(w_loaded, 16)
            sp.dma_start(w_in[:, 4, :], ffn_V).then_inc(w_loaded, 16)
            sp.dma_start(gamma_row[:, :], gamma_k.rearrange("h d -> (h d)").partition_broadcast(P)).then_inc(w_loaded, 16)
            sp.dma_start(beta_row[:, :], beta_k.rearrange("(a h) d -> a (h d)", a=1)).then_inc(w_loaded, 16)
            sp.dma_start(bn_gamma[:, :], ffn_gamma.rearrange("(p a) -> p a", a=1)).then_inc(w_loaded, 16)
            sp.dma_start(bn_beta[:, :], ffn_beta.rearrange("(p a) -> p a", a=1)).then_inc(w_loaded, 16)

            for j in range(RING):
                load_x(0, j, j)

            def refill_a(b, i):
                for j in range(RING):
                    wait_alone(sp, "sp", a_gram, b * (GB * NQ) + i * (RING * NQ) + (j + 1 - RING) * NQ + PRIMED)
                    load_x(b, i * RING + j, j)

            with sp.Fori(1, BODIES) as i:
                refill_a(0, i)
            with sp.Fori(1, B) as b:
                with sp.Fori(0, BODIES) as i:
                    refill_a(b, i)
            for j in range(RING):
                sp.wait_ge(a_gram, B * GB * NQ + (j + 1 - RING) * NQ + PRIMED)
                load_x(0, j, j)

            def step_b(b, i, load):
                for j in range(RING):
                    group = b * GB + i * RING + j
                    wait_alone(sp, "sp", b_x2, (group + 1) * DQ)
                    wait_alone(sp, "sp", b_added, group + 1)
                    load(j)
                    sp.dma_start(
                        x2_dram[bass.ds((i * RING + j) * (GT // LT), GT // LT), :, b, :].rearrange("k p f -> p k f"),
                        x2g[:, j, :].rearrange("p (k f) -> p k f", f=LT * C)).then_inc(x2_stored[j], 16)

            with sp.Fori(0, B - 1) as b:
                with sp.Fori(0, BODIES - 1) as i:
                    step_b(b, i, lambda j: load_x(b, (i + 1) * RING + j, j))
                step_b(b, BODIES - 1, lambda j: load_x(b + 1, j, j))
            with sp.Fori(0, BODIES - 1) as i:
                step_b(B - 1, i, lambda j: load_x(B - 1, (i + 1) * RING + j, j))
            step_b(B - 1, BODIES - 1, lambda j: None)
            for j in range(RING):
                sp.wait_ge(x2_stored[j], 16 * (B * BODIES + PRIMED))

            def load_x2(k, part):
                sp.dma_start(xg[:, part, :],
                             x2_dram[bass.ds(k * PARTS + part, 1), :, :, :].rearrange("a p b f -> p (a b f)")
                             ).then_inc(x2_in[part], 16)

            def step_c(n, k, k_next):
                for part in range(PARTS):
                    wait_alone(sp, "sp", c_out, n * BT + (part + 1) * LT)
                    load_x2(k_next, part)
                    sp.dma_start(out_g[:, :, bass.ds(k * (BT * C) + part * (LT * C), LT * C)],
                                 x2g[:, part, :].rearrange("p (b f) -> p b f", b=B)).then_inc(out_stored[part], 16)

            sp.wait_ge(b_T, B * GB * NQ)
            for part in range(PARTS):
                load_x2(CB - 1, part)
            step_c(0, CB - 1, 0)
            limit = sp.alloc_register("sp_limit")
            sp.reg_mov(limit, 1)
            with sp.Fori(0, limit) as r:
                with sp.Fori(0, CB - 1) as k:
                    step_c(r * CB + k + 1, k, k + 1)
                step_c(r * CB + CB, CB - 1, 0)
                for part in range(PARTS):
                    wait_alone(sp, "sp", out_stored[part], r * (16 * CB) + 16 * (CB + 1))
                    wait_alone(sp, "sp", x2_in[part], r * (16 * CB) + 16 * (CB + 2))
                wait_alone(sp, "sp", verdict, r + 1)
                sp.reg_load(limit, rounds_limit[0:1, 0:1])

        @block.tensor
        def _(pe):
            pe.wait_ge(w_loaded, 16 * 9)
            pe.wait_ge(consts_done, 1)
            for n in range(3):
                last = nc.tensor.matmul(pM[:, n * P:(n + 1) * P], center[:, :], w_in[:, n, :], start=True, stop=True)
            last.then_inc(setup_pe, 1)
            nc.tensor.transpose(pT[:, 0, 0:P], w_in[:, 4, :], ident[:, :]).then_inc(setup_pe, 1)
            pe.wait_ge(setup_dve, 1)
            nc.tensor.transpose(pT[:, 1, 0:P], w_c[:, 0, :], ident[:, :]).then_inc(setup_pe, 1)
            pe.wait_ge(setup_dve, 2)
            nc.tensor.transpose(pG[:, 0:P], f_c[:, :], ident[:, :]).then_inc(setup_pe, 1)
            pe.wait_ge(setup_done, 1)

            def transposes(src, s_T, s_xT, j, c, q, first=False, loads=None):
                if loads is not None:
                    pe.wait_ge(x_in[j], loads)
                if not first:
                    pe.wait_ge(s_xT, q - 1)
                for t in range(QT):
                    last = nc.tensor.transpose(pT[:, c % 2, t * P:(t + 1) * P], tile(src, j, c * QT + t), ident[:, :])
                last.then_inc(s_T, 1)

            def group_a(j, q0, first=False):
                for c in range(2, NQ):
                    transposes(xg, a_T, a_lo, j, c, q0 + c)
                for c in range(NQ):
                    q = q0 + c
                    pe.wait_ge(a_lo, q + 1)
                    for t in range(QT):
                        if t == 0 and not (first and c < 2):
                            pe.wait_ge(a_z_read, q - 1)
                        if t == 2 and not (first and c < 2):
                            pe.wait_ge(a_sq, q - 1)
                        z = pZ[:, c % 2, t // 2, (t % 2) * 2 * P:(t % 2 + 1) * 2 * P]
                        hi, lo = (part[:, c % 4, t * P:(t + 1) * P] for part in (xT_hi, xT_lo))
                        nc.tensor.matmul(z, hi, w_kv_hi[:, t // 2, :], start=True, stop=False)
                        nc.tensor.matmul(z, hi, w_kv_lo[:, t // 2, :], start=False, stop=False)
                        last = nc.tensor.matmul(z, lo, w_kv_hi[:, t // 2, :], start=False, stop=True)
                    last.then_inc(a_z, 1)

            def gram_quad(s_xs, s_gram, src, ring, width, j, c, need):
                pe.wait_ge(s_xs, need)
                for t in range(QT):
                    last = nc.tensor.matmul(pG[:, 0:width], tile(src, j, c * QT + t),
                                            xs[:, ring, c * QT + t, 0:width], start=False, stop=False,
                                            skip_group_check=True)
                last.then_inc(s_gram, 1)

            def open_gram(width):
                return nc.tensor.matmul(pG[:, 0:width], zeros[:, 0:P], zeros[:, 0:width], start=True, stop=False,
                                        skip_group_check=True)

            transposes(xg, a_T, a_lo, 0, 0, 0, first=True, loads=16)
            transposes(xg, a_T, a_lo, 0, 1, 1, first=True)
            group_a(0, 0, first=True)
            transposes(xg, a_T, a_lo, 1, 0, NQ, loads=16)
            transposes(xg, a_T, a_lo, 1, 1, NQ + 1)
            open_gram(C + 2).then_inc(a_gram, PRIMED)
            with pe.Fori(0, B) as b:
                pe.wait_ge(gram_saved, b + PRIMED)
                open_gram(C + 2)
                with pe.Fori(0, BODIES) as i:
                    n = pe.snap(b * BODIES + i)
                    q0 = pe.snap(n * (RING * NQ))
                    for j in range(RING):
                        j1, j2 = (j + 1) % RING, (j + 2) % RING
                        group_a(j1, q0 + (j + 1) * NQ)
                        for c in range(NQ):
                            gram_quad(a_xs, a_gram, xg, j % 2, C + 2, j, c, q0 + j * NQ + c + 1)
                            if c < 2:
                                transposes(xg, a_T, a_lo, j2, c, q0 + (j + 2) * NQ + c,
                                           loads=n * 16 + 16 * (1 + (j + 2) // RING))

            pe.wait_ge(gram_saved, B + PRIMED)
            pe.wait_ge(a_lo, (B * GB + 1) * NQ + 2)
            for b in range(B):
                last = nc.tensor.matmul(pM[:, b * P:(b + 1) * P], gram[:, b, 0:C], w_kvg[:, 1, :], start=True, stop=True)
            last.then_inc(setup_pe, 1)
            for n in range(2):
                for b in range(B):
                    last = nc.tensor.matmul(pT[0:1, n, b * P:(b + 1) * P], gram[:, b, C + n:C + n + 1],
                                            w_kvg[:, n, :], start=True, stop=True)
            last.then_inc(setup_pe, 1)
            pe.wait_ge(setup_dve, 3)
            nc.tensor.matmul(pZ[:, 0, 0, :], w_kvg[:, 0, :], gram_v[:, :, :].rearrange("p b c -> p (b c)"),
                             start=True, stop=False, skip_group_check=True)
            for b in range(B):
                nc.tensor.matmul(pZ[:, 0, 0, b * P:(b + 1) * P], rows[0:1, 0, b, :], beta_row[:, :],
                                 start=False, stop=False, skip_group_check=True)
            nc.tensor.matmul(pZ[:, 0, 0, :], beta_row[:, :], rows[0:1, 1, :, :].rearrange("a b c -> a (b c)"),
                             start=False, stop=True, skip_group_check=True).then_inc(setup_pe, 1)
            pe.wait_ge(setup_dve, 4)
            nc.tensor.matmul(pM[:, :], w_qT[:, :], kv_heads[:, :, :].rearrange("p b c -> p (b c)"),
                             start=True, stop=True).then_inc(setup_pe, 1)
            pe.wait_ge(setup_dve, 5)

            def group_b(j, g, q0, first=False):
                m_now = m_all[:, bass.ds(pe.snap(g // GB) * P, P)] if not isinstance(g, int) else \
                    m_all[:, g // GB * P:(g // GB + 1) * P]
                for c in range(2, NQ):
                    transposes(xg, b_T, b_xT, j, c, q0 + c)
                for c in range(NQ):
                    q = q0 + c
                    pe.wait_ge(b_xT, q + 1)
                    if c == DQ and not first:
                        pe.wait_ge(b_scaled, g)
                    elif not first:
                        pe.wait_ge(b_x2, (g - 1) * DQ + c + 1)
                    for t in range(QT):
                        last = nc.tensor.matmul(pZ[:, c % 2, c // 2, t * P:(t + 1) * P],
                                                xT[:, c % 4, t * P:(t + 1) * P], m_now, start=True, stop=True)
                    last.then_inc(b_u, 1)

            A_LOADS = 16 * B * BODIES
            def front_b(j, g, q0, loads, c):
                transposes(xg, b_T, b_xT, j, c, q0 + c, first=isinstance(g, int) and g == 0, loads=loads)

            def body_b(n):
                peeled = isinstance(n, int)
                q0 = n * (RING * NQ) if peeled else pe.snap(n * (RING * NQ))
                g0 = n * RING if peeled else pe.snap(n * RING)
                for j in range(RING):
                    if not (peeled and g0 + j + 2 >= B * GB):
                        group_b((j + 2) % RING, g0 + (j + 2), q0 + (j + 2) * NQ)
                    for c in range(NQ):
                        if c < 2 and not (peeled and g0 + j + 3 >= B * GB):
                            front_b((j + 3) % RING, g0 + (j + 3), q0 + (j + 3) * NQ,
                                    n * 16 + A_LOADS + 16 * (1 + (j + 3) // RING), c)
                        gram_quad(b_xs, b_gram, x2g, j % 2, C + 1, j, c, q0 + j * NQ + c + 1)

            for g in range(2):
                for c in range(2):
                    front_b(g, g, g * NQ, A_LOADS + 16, c)
                group_b(g, g, g * NQ, first=g == 0)
            for c in range(2):
                front_b(2, 2, 2 * NQ, A_LOADS + 16, c)
            open_gram(C + 1)
            with pe.Fori(0, B * BODIES - 1) as n:
                body_b(n)
            body_b(B * BODIES - 1)

            pe.wait_ge(gram_saved, B + 1 + PRIMED)
            nc.tensor.matmul(pM[:, 0:P], f_cT[:, :], gram2[:, 0:C], start=True, stop=True)
            nc.tensor.matmul(pM[:, P:P + 1], f_cT[:, :], gram2[:, C:C + 1], start=True, stop=True).then_inc(setup_pe, 1)
            pe.wait_ge(setup_dve, 6)
            nc.tensor.transpose(pM[:, 0:P], f_scaled[:, :], ident[:, :]).then_inc(setup_pe, 1)
            pe.wait_ge(setup_dve, 7)
            pe.wait_ge(b_xT, B * GB * NQ)

            def forward(s, ring):
                pe.wait_ge(c_xn, s + 1)
                wait_pos(pe, c_lo, s - 1)
                for b in range(B):
                    last = nc.tensor.transpose(pT[:, ring % 2, b * P:(b + 1) * P], xn[:, ring % 4, b, :], ident[:, :])
                last.then_inc(c_T, 1)

            def project(s, ring):
                pe.wait_ge(c_lo, s + 1)
                pre = pZ[:, 0, ring % 2, :]
                nc.tensor.matmul(pre, f_hi[:, :], xT_hi[:, ring % 2, :], start=True, stop=False, skip_group_check=True)
                nc.tensor.matmul(pre, f_lo[:, :], xT_hi[:, ring % 2, :], start=False, stop=False, skip_group_check=True)
                nc.tensor.matmul(pre, f_hi[:, :], xT_lo[:, ring % 2, :], start=False, stop=False,
                                 skip_group_check=True).then_inc(c_w, 1)

            def recur(s, ring):
                nc.tensor.matmul(pZ[:, 0, ring % 2, :], v_T[:, :], y[:, (ring + 3) % 4, :], start=False, stop=True,
                                 skip_group_check=True).then_inc(c_pre, 1)

            def back(s, ring):
                pe.wait_ge(c_y, s + 1)
                wait_pos(pe, c_out, s - 1)
                for b in range(B):
                    last = nc.tensor.transpose(pZ[:, 1, ring % 2, b * P:(b + 1) * P], y[:, ring % 4, b * P:(b + 1) * P],
                                               ident[:, :])
                last.then_inc(c_back, 1)

            def body_c(n, enter):
                s0 = n * BT if isinstance(n, int) else pe.snap(n * BT)
                for t in range(BT):
                    if t or not enter:
                        pe.wait_ge(c_y, s0 + t)
                    recur(s0 + t, t)
                    forward(s0 + t + 2, t + 2)
                    project(s0 + t + 1, t + 1)
                    back(s0 + t, t)

            forward(0, 0)
            forward(1, 1)
            project(0, 0)
            pe.wait_ge(entry_set, 1)
            body_c(0, True)
            limit = pe.alloc_register("pe_limit")
            pe.reg_mov(limit, 1)
            with pe.Fori(0, limit) as r:
                wait_alone(pe, "pe", entry_set, r + 2)
                with pe.Fori(0, CB) as k:
                    body_c(r * CB + k + 1, False)
                wait_alone(pe, "pe", verdict, r + 1)
                pe.reg_load(limit, rounds_limit[0:1, 0:1])

        @block.scalar
        def _(act):
            def copy_quad(dst, s_T, s_z, s_xT, q, c, first=False):
                act.wait_ge(s_T, q + 1)
                if not first:
                    act.wait_ge(s_z, q - 3)
                nc.scalar.activation(dst[:, c % 4, :], pT[:, c % 2, :], ACT.Copy).then_inc(s_xT, 1)

            def roots(s_var, s_std, par, g, width):
                act.wait_ge(s_var, g + 1)
                nc.scalar.activation(std_c[:, par, :, 0:width], var_c[:, par, :, 0:width], ACT.Sqrt).then_inc(s_std, 1)

            def squares(q, c, par, first=False):
                act.wait_ge(a_z, q + 1)
                for t in range(2):
                    for kv in range(2):
                        z = pZ[:, c % 2, 1, (2 * t + kv) * P:(2 * t + kv + 1) * P]
                        last = nc.scalar.activation(z, z, ACT.Square, accum_out=z_sq[:, par, c, t, kv:kv + 1])
                last.then_inc(a_sq, 1)

            def group_a(q0, g, par, first=False):
                for c in range(2, NQ):
                    copy_quad(xT_hi, a_T, a_z, a_hi, q0 + c, c, first=first)
                for c in range(NQ):
                    squares(q0 + c, c, par)
                for c in range(2):
                    copy_quad(xT_hi, a_T, a_z, a_hi, q0 + NQ + c, c)
                roots(a_var, a_std, par, g, 3)

            for q in range(2):
                copy_quad(xT_hi, a_T, a_z, a_hi, q, q, first=True)
            group_a(0, 0, 0, first=True)
            with act.Fori(0, B) as b:
                with act.Fori(0, BODIES) as i:
                    n = act.snap(b * BODIES + i)
                    q0 = act.snap(n * (RING * NQ))
                    g0 = act.snap(n * RING)
                    for j in range(RING):
                        group_a(q0 + (j + 1) * NQ, g0 + (j + 1), (j + 1) % 2)
                act.wait_ge(a_gram, b * (GB * NQ) + GB * NQ + PRIMED)
                nc.scalar.activation(gram[:, bass.ds(b, 1), :].rearrange("p a c -> p (a c)"), pG[:, 0:C + 2],
                                     ACT.Copy).then_inc(gram_saved, 1)

            act.wait_ge(setup_dve, 5)

            def group_b(j, g, q0, stores):
                known = isinstance(g, int)
                par = j % 2
                if not (known and g == 0):
                    roots(b_var, b_std, 1 - par, g - 1, 1)
                for c in range(2, NQ):
                    copy_quad(xT, b_T, b_u, b_xT, q0 + c, c, first=known and g == 0)
                act.wait_ge(x2_stored[j], stores)
                act.wait_ge(b_gram, q0 + NQ)
                act.wait_ge(b_r1, g + 1)
                act.wait_ge(b_u, q0 + NQ)
                for tt in range(DQ * QT, NQ * QT):
                    last = nc.scalar.activation(tile(x2g, j, tt), pZ[:, DQ % 2, DQ // 2, (tt % QT) * P:(tt % QT + 1) * P],
                                                ACT.Copy, scale=r1_now[:, par, tt:tt + 1])
                last.then_inc(b_scaled, 1)
                if not (known and g == B * GB - 1):
                    for c in range(2):
                        copy_quad(xT, b_T, b_u, b_xT, q0 + NQ + c, c)

            for q in range(2):
                copy_quad(xT, b_T, b_u, b_xT, q, q, first=True)
            for g in range(2):
                group_b(g, g, g * NQ, 16 * PRIMED)
            with act.Fori(0, B * BODIES - 1) as n:
                q0 = act.snap(n * (RING * NQ))
                g0 = act.snap(n * RING)
                for j in range(2, RING + 2):
                    group_b(j % RING, g0 + j, q0 + j * NQ, n * 16 + 16 * (j // RING + PRIMED))
            for g in range(B * GB - 2, B * GB):
                group_b(g % RING, g, g * NQ, 16 * (g // RING + PRIMED))
            roots(b_var, b_std, (B * GB - 1) % 2, B * GB - 1, 1)
            act.wait_ge(b_gram, (B * GB + RING) * NQ)
            nc.scalar.activation(gram2[:, :], pG[:, 0:C + 1], ACT.Copy).then_inc(gram_saved, 1)

            act.wait_ge(bn_var, 1)
            nc.scalar.activation(bn_cols[:, 6:7], bn_cols[:, 5:6], ACT.Sqrt).then_inc(bn_std, 1)

            def take_forward(s, ring):
                act.wait_ge(c_T, s + 1)
                wait_pos(act, c_w, s - 1)
                nc.scalar.activation(xT_hi[:, ring % 2, :], pT[:, ring % 2, :], ACT.Copy).then_inc(c_hi, 1)

            def body_c(n):
                s0 = n * BT if isinstance(n, int) else act.snap(n * BT)
                for t in range(BT):
                    act.wait_ge(c_pre, s0 + t + 1)
                    nc.scalar.activation(y[:, t % 4, :], pZ[:, 0, t % 2, :], ACT.Sigmoid,
                                         bias=bn_cols[:, 7:8]).then_inc(c_y, 1)
                    take_forward(s0 + t + 2, t + 2)

            act.wait_ge(setup_dve, 7)
            take_forward(0, 0)
            take_forward(1, 1)
            body_c(0)
            limit = act.alloc_register("act_limit")
            act.reg_mov(limit, 1)
            with act.Fori(0, limit) as r:
                with act.Fori(0, CB) as k:
                    body_c(r * CB + k + 1)
                wait_alone(act, "act", verdict, r + 1)
                act.reg_load(limit, rounds_limit[0:1, 0:1])

        @block.vector
        def _(dve):
            chain = [0]

            def link(ins):
                chain[0] += 1
                ins.then_inc(dve_chain, 1)
                dve.wait_ge(dve_chain, chain[0])

            dve.wait_ge(w_loaded, 16 * 9)
            dve.wait_ge(consts_done, 1)
            dve.wait_ge(setup_pe, 1)
            nc.vector.tensor_copy(w_kv[:, 0, 0:2 * P:2], pM[:, P:2 * P])
            nc.vector.tensor_copy(w_kv[:, 0, 1:2 * P:2], pM[:, 2 * P:3 * P])
            nc.vector.tensor_copy(w_c[:, :, :].rearrange("p a b -> p (a b)"), pM[:, 0:3 * P]).then_inc(setup_dve, 1)
            dve.wait_ge(setup_dve, 1)
            link(nc.vector.tensor_reduce(w_mean[:, :], w_c[:, :, :], AX.X, ALU.add))
            link(nc.vector.tensor_scalar(w_mean[:, :], w_mean[:, :], 1.0 / P, None, ALU.mult))
            for n in range(2):
                nc.vector.scalar_tensor_tensor(w_kvg[:, n, :], w_c[:, 1 + n, :], w_mean[:, 1 + n:2 + n], gamma_row[:, :],
                                               ALU.subtract, ALU.mult)
                nc.vector.tensor_scalar(w_kv[:, 1, n * P:(n + 1) * P], w_c[:, 1 + n, :], w_mean[:, 1 + n:2 + n], None,
                                        ALU.subtract)
            link(nc.vector.tensor_reduce(bn_cols[:, 0:1], w_in[:, 3, :], AX.X, ALU.add))
            link(nc.vector.tensor_copy(w_kv_hi[:, :, :], w_kv[:, :, :]))
            nc.vector.tensor_tensor(w_kv_lo[:, :, :], w_kv[:, :, :], w_kv_hi[:, :, :].bitcast(F32), ALU.subtract)
            link(nc.vector.tensor_scalar(bn_cols[:, 1:2], bn_cols[:, 0:1], 1.0 / P, None, ALU.mult))
            nc.vector.tensor_scalar(f_c[:, :], w_in[:, 3, :], bn_cols[:, 1:2], None, ALU.subtract).then_inc(setup_dve, 1)
            dve.wait_ge(setup_pe, 3)
            nc.vector.tensor_copy(v_T[:, :], pT[:, 0, 0:P])
            nc.vector.tensor_copy(w_qT[:, :], pT[:, 1, 0:P])
            dve.wait_ge(setup_pe, 4)
            nc.vector.tensor_copy(f_cT[:, :], pG[:, 0:P]).then_inc(setup_done, 1)
            nc.vector.memset(kv_heads[:, :, :], 0.0)
            nc.vector.memset(entry_next[:, :], 0.0)
            nc.vector.memset(y[:, 3, :], 0.0).then_inc(entry_set, 1)
            nc.vector.memset(entry[:, :], 0.0).then_inc(gram_saved, PRIMED)

            def var_of_x(s_small, par, base, eps):
                dve.wait_ge(s_small, base + 1)
                nc.vector.tensor_tensor(mean_gap[:, :, :], x_stats[:, par, :, 1:2], x_stats[:, par, :, 4:5], ALU.subtract)
                nc.vector.scalar_tensor_tensor(sum_sq[:, :, :], x_stats[:, par, :, 2:3], C * eps, x_stats[:, par, :, 5:6],
                                               ALU.add, ALU.add).then_inc(s_small, 1)
                dve.wait_ge(s_small, base + 2)
                nc.vector.scalar_tensor_tensor(gap_sq[:, :, :], mean_gap[:, :, :], C / 4.0, mean_gap[:, :, :],
                                               ALU.mult, ALU.mult).then_inc(s_small, 1)
                dve.wait_ge(s_small, base + 3)
                return nc.vector.tensor_tensor(var_c[:, par, :, 0:1], sum_sq[:, :, :], gap_sq[:, :, :], ALU.add)

            def reciprocals(s_std, s_rstd, par, g, width):
                dve.wait_ge(s_std, g + 1)
                nc.vector.reciprocal(rstd_c[:, par, :, 0:width], std_c[:, par, :, 0:width]).then_inc(s_rstd, 1)

            by_quad = lambda ap: ap.rearrange("p (c t) w -> p c t w", c=NQ)

            def take_low(q, c, first=False):
                dve.wait_ge(a_hi, q + 1)
                if not first:
                    dve.wait_ge(a_z, q - 3)
                nc.vector.tensor_tensor(xT_lo[:, c % 4, :], pT[:, c % 2, :], xT_hi[:, c % 4, :].bitcast(F32),
                                        ALU.subtract).then_inc(a_lo, 1)

            def stats_of_x(j, par, first_tile, count):
                for t in range(first_tile, first_tile + count):
                    last = nc.vector.bn_stats(x_stats[:, par, t, :], tile(xg, j, t))
                return last

            def group_a(j, par, q0, g, loads, first=False):
                j_next = (j + 1) % RING

                def stats_of_z(c):
                    dve.wait_ge(a_z, q0 + c + 1)
                    for t in range(2):
                        last = nc.vector.bn_stats(z_stats[:, c, t, :], pZ[:, c % 2, 0, t * 2 * P:(t + 1) * 2 * P])
                    last.then_inc(a_z_read, 1)

                if not first:
                    dve.wait_ge(a_var, g)
                dve.wait_ge(x_in[j_next], loads)
                stats_of_x(j_next, 1 - par, 0, 2)
                take_low(q0 + 2, 2, first=first)
                if not first:
                    reciprocals(a_std, a_rstd, 1 - par, g - 1, 3)
                stats_of_z(0)
                take_low(q0 + 3, 3, first=first)
                stats_of_z(1)
                stats_of_x(j_next, 1 - par, 2, 3)
                stats_of_z(2)
                stats_of_x(j_next, 1 - par, 5, 3)
                stats_of_z(3)
                stats_of_x(j_next, 1 - par, 8, 1)
                if not first:
                    dve.wait_ge(a_var_read, g - 2 + 1 + PRIMED)
                var_of_x(a_small, par, g * 4, LN_C_EPS).then_inc(a_small, 1)
                dve.wait_ge(a_small, g * 4 + 4)
                dve.wait_ge(a_z_read, q0 + NQ)
                dve.wait_ge(a_sq, q0 + NQ)
                var_q = by_quad(var_c[:, par, :, :])
                for kv in range(2):
                    for pair, m2 in ((slice(0, 2), z_stats[:, :, :, 2 + 3 * kv]), (slice(2, 4), z_sq[:, par, :, :, kv])):
                        last = nc.vector.scalar_tensor_tensor(var_q[:, :, pair, 1 + kv], var_q[:, :, pair, 0], HD_EPS, m2,
                                                              ALU.mult, ALU.add)
                last.then_inc(a_var, 1)
                take_low(q0 + NQ, 0)
                stats_of_x(j_next, 1 - par, 9, 3)
                take_low(q0 + NQ + 1, 1)
                stats_of_x(j_next, 1 - par, 12, 4).then_inc(a_small, 1)

            take_low(0, 0, first=True)
            take_low(1, 1, first=True)
            dve.wait_ge(x_in[0], 16)
            stats_of_x(0, 0, 0, GT).then_inc(a_small, 1)
            group_a(0, 0, 0, 0, 16, first=True)
            with dve.Fori(0, B * BODIES) as n:
                q0 = dve.snap(n * (RING * NQ))
                g0 = dve.snap(n * RING)
                for j in range(RING):
                    group_a((j + 1) % RING, (j + 1) % 2, q0 + (j + 1) * NQ, g0 + (j + 1),
                            n * 16 + 16 * (1 + (j + 2) // RING))
            reciprocals(a_std, a_rstd, 0, B * GB, 3)

            dve.wait_ge(setup_pe, 5)
            nc.vector.tensor_copy(gram_v[:, :, :].rearrange("p b c -> p (b c)"), pM[:, :])
            dve.wait_ge(setup_pe, 6)
            nc.vector.scalar_tensor_tensor(rows[:, 0, :, :], beta_row[:, :].unsqueeze(1).to_broadcast([1, B, P]), float(N),
                                           pT[0:1, 0, :].rearrange("a (b c) -> a b c", b=B), ALU.mult, ALU.add)
            nc.vector.tensor_copy(rows[:, 1, :, :], pT[0:1, 1, :].rearrange("a (b c) -> a b c", b=B)).then_inc(setup_dve, 1)
            dve.wait_ge(setup_pe, 7)
            for h in range(HEADS):
                hs = slice(h * HD, (h + 1) * HD)
                last = nc.vector.tensor_scalar(kv_heads[hs, :, hs],
                                               pZ[:, 0, 0, :].rearrange("p (b c) -> p b c", b=B)[hs, :, hs],
                                               1.0 / N, None, ALU.mult)
            last.then_inc(setup_dve, 1)
            dve.wait_ge(setup_pe, 8)
            nc.vector.tensor_copy(m_all[:, :].rearrange("p (b e h) -> p b h e", b=B, h=HEADS),
                                  pM[:, :].rearrange("p (b h e) -> p b h e", b=B, h=HEADS)).then_inc(setup_dve, 1)

            def group_b(j, g, q0, loads, stores):
                par = j % 2
                first = isinstance(g, int) and g == 0
                if not first:
                    reciprocals(b_std, b_rstd, 1 - par, g - 1, 1)
                nc.vector.tensor_copy(r1_now[:, par, :], r1_all[:, bass.ds(g * GT, GT)]).then_inc(b_r1, 1)
                dve.wait_ge(b_r1, g + 1)
                dve.wait_ge(x_in[j], loads)
                dve.wait_ge(x2_stored[j], stores)
                dve.wait_ge(b_gram, q0 + NQ)
                if not first:
                    dve.wait_ge(b_var, g)

                def stats(c):
                    if c < DQ:
                        dve.wait_ge(b_x2, g * DQ + c + 1)
                    else:
                        dve.wait_ge(b_added, g + 1)
                    for t in range(QT):
                        last = nc.vector.bn_stats(x_stats[:, par, c * QT + t, :], tile(x2g, j, c * QT + t))
                    return last

                for c in range(DQ):
                    dve.wait_ge(b_u, q0 + c + 1)
                    for t in range(QT):
                        tt = c * QT + t
                        last = nc.vector.scalar_tensor_tensor(
                            tile(x2g, j, tt), pZ[:, c % 2, c // 2, t * P:(t + 1) * P], r1_now[:, par, tt:tt + 1],
                            tile(xg, j, tt), ALU.mult, ALU.add)
                    last.then_inc(b_x2, 1)
                    if c:
                        stats(c - 1)
                stats(DQ - 1)
                stats(NQ - 1).then_inc(b_small, 1)
                if not first:
                    dve.wait_ge(b_var_read, g - 2 + 1 + PRIMED)
                var_of_x(b_small, par, g * 3, LN_T_EPS).then_inc(b_var, 1)

            A_LOADS = 16 * B * BODIES
            dve.wait_ge(a_xs, (B * GB + 1) * NQ)
            for g in range(2):
                group_b(g, g, g * NQ, A_LOADS + 16, 16 * PRIMED)
            with dve.Fori(0, B * BODIES - 1) as n:
                q0 = dve.snap(n * (RING * NQ))
                g0 = dve.snap(n * RING)
                for j in range(2, RING + 2):
                    body = j // RING
                    group_b(j % RING, g0 + j, q0 + j * NQ, n * 16 + A_LOADS + 16 * (1 + body),
                            n * 16 + 16 * (body + PRIMED))
            for g in range(B * GB - 2, B * GB):
                group_b(g % RING, g, g * NQ, A_LOADS + 16 * (1 + g // RING), 16 * (g // RING + PRIMED))
            reciprocals(b_std, b_rstd, (B * GB - 1) % 2, B * GB - 1, 1)

            dve.wait_ge(setup_pe, 9)
            link(nc.vector.tensor_tensor(bn_prod[:, :], pM[:, 0:P], f_c[:, :], ALU.mult))
            nc.vector.tensor_scalar(bn_cols[:, 3:4], pM[:, P:P + 1], 1.0 / (B * N), None, ALU.mult)
            link(nc.vector.tensor_reduce(bn_cols[:, 2:3], bn_prod[:, :], AX.X, ALU.add))
            link(nc.vector.tensor_tensor(bn_cols[:, 4:5], bn_cols[:, 3:4], bn_cols[:, 3:4], ALU.mult))
            link(nc.vector.scalar_tensor_tensor(bn_cols[:, 5:6], bn_cols[:, 2:3], 1.0 / (B * N), bn_cols[:, 4:5],
                                                ALU.mult, ALU.subtract))
            nc.vector.tensor_scalar(bn_cols[:, 5:6], bn_cols[:, 5:6], BN_EPS, None, ALU.add).then_inc(bn_var, 1)
            dve.wait_ge(bn_std, 1)
            link(nc.vector.reciprocal(bn_cols[:, 0:1], bn_cols[:, 6:7]))
            link(nc.vector.tensor_tensor(bn_cols[:, 1:2], bn_cols[:, 0:1], bn_cols[:, 0:1], ALU.mult))
            link(nc.vector.tensor_tensor(bn_cols[:, 2:3], bn_cols[:, 1:2], bn_cols[:, 5:6], ALU.mult))
            link(nc.vector.tensor_scalar(bn_cols[:, 4:5], bn_cols[:, 2:3], -0.5, 1.5, ALU.mult, ALU.add))
            link(nc.vector.tensor_tensor(bn_cols[:, 6:7], bn_cols[:, 0:1], bn_cols[:, 4:5], ALU.mult))
            link(nc.vector.tensor_tensor(bn_cols[:, 0:1], bn_cols[:, 6:7], bn_gamma[:, :], ALU.mult))
            link(nc.vector.tensor_tensor(bn_cols[:, 1:2], bn_cols[:, 3:4], bn_cols[:, 0:1], ALU.mult))
            nc.vector.tensor_tensor(bn_cols[:, 7:8], bn_beta[:, :], bn_cols[:, 1:2], ALU.subtract)
            nc.vector.tensor_scalar(f_scaled[:, :], f_c[:, :], bn_cols[:, 0:1], None, ALU.mult).then_inc(setup_dve, 1)
            dve.wait_ge(setup_pe, 10)
            link(nc.vector.tensor_copy(f_scaledT[:, :], pM[:, 0:P]))
            link(nc.vector.tensor_copy(f_hi[:, :], f_scaledT[:, :]))
            nc.vector.tensor_tensor(f_lo[:, :], f_scaledT[:, :], f_hi[:, :].bitcast(F32), ALU.subtract).then_inc(setup_dve, 1)

            x2_part = xg[:, :, :].rearrange("p l (b t c) -> p l b t c", b=B, c=C)
            out_part = x2g[:, :, :].rearrange("p l (b t c) -> p l b t c", b=B, c=C)

            def take_forward(s, ring):
                dve.wait_ge(c_hi, s + 1)
                nc.vector.tensor_tensor(xT_lo[:, ring % 2, :], pT[:, ring % 2, :], xT_hi[:, ring % 2, :].bitcast(F32),
                                        ALU.subtract).then_inc(c_lo, 1)

            def body_c(n):
                s0 = n * BT if isinstance(n, int) else dve.snap(n * BT)
                for t in range(BT):
                    part = t // LT
                    take_forward(s0 + t + 2, t + 2)
                    if t % LT == 0:
                        wait_pos(dve, out_stored[part], n * 16)
                    dve.wait_ge(c_back, s0 + t + 1)
                    nc.vector.tensor_tensor(out_part[:, part, :, t % LT, :],
                                            pZ[:, 1, t % 2, :].rearrange("p (b c) -> p b c", b=B),
                                            x2_part[:, part, :, t % LT, :], ALU.add).then_inc(c_out, 1)

            by_batch = lambda ap: ap.rearrange("p (b c) -> p b c", b=B)

            dve.wait_ge(b_xs, B * GB * NQ)
            take_forward(0, 0)
            take_forward(1, 1)
            body_c(0)
            link(nc.vector.tensor_copy(by_batch(entry_next[:, :])[:, :, 1:P], by_batch(y[:, 3, :])[:, :, 0:P - 1]))
            nc.vector.tensor_copy(entry[:, :], entry_next[:, :])
            nc.vector.tensor_copy(y[:, 3, :], entry_next[:, :]).then_inc(entry_set, 1)
            limit = dve.alloc_register("dve_limit")
            dve.reg_mov(limit, 1)
            with dve.Fori(0, limit) as r:
                with dve.Fori(0, CB) as k:
                    body_c(r * CB + k + 1)
                nc.vector.tensor_copy(by_batch(entry_next[:, :])[:, :, 1:P],
                                      by_batch(y[:, 3, :])[:, :, 0:P - 1]).then_inc(c_chain, 1)
                dve.wait_ge(c_chain, r * 2 + 1)
                nc.vector.tensor_tensor(entry_diff[:, :], entry_next[:, :], entry[:, :], ALU.subtract).then_inc(c_chain, 1)
                dve.wait_ge(c_chain, r * 2 + 2)
                nc.vector.tensor_reduce(diff_max[:, :], entry_diff[:, :], AX.X, ALU.max,
                                        apply_absolute_value=True).then_inc(diff_ready, 1)
                nc.vector.tensor_copy(entry[:, :], entry_next[:, :])
                nc.vector.tensor_copy(y[:, 3, :], entry_next[:, :]).then_inc(entry_set, 1)
                dve.wait_ge(diff_reduced, r + 1)
                nc.vector.tensor_scalar(rounds_limit[:, :], diff_all[:, :], SETTLED, float(P), ALU.is_gt,
                                        ALU.mult).then_inc(verdict, 1)
                wait_alone(dve, "dve", verdict, r + 1)
                dve.reg_load(limit, rounds_limit[0:1, 0:1])

        @block.gpsimd
        def _(pool):
            nc.gpsimd.memset(ident[:, :], 0.0).then_inc(ident_made, 1)
            nc.gpsimd.memset(zeros[:, :], 0.0)
            pool.wait_ge(ident_made, 1)
            nc.gpsimd.affine_select(out=ident[:, :], in_=ident[:, :], compare_op=ALU.not_equal, fill=1.0, base=0,
                                    pattern=[[-1, P]], channel_multiplier=1).then_inc(ident_made, 1)
            pool.wait_ge(ident_made, 2)
            nc.gpsimd.tensor_scalar(center[:, :], ident[:, :], -1.0 / C, None, ALU.add).then_inc(consts_done, 1)
            pool.sem_inc(a_var_read, PRIMED)
            pool.sem_inc(b_var_read, PRIMED)
            pool.sem_inc(b_gram, RING * NQ)
            for j in range(RING):
                pool.sem_inc(x2_stored[j], 16 * PRIMED)

            def scale_quads(src, j, par, s_xs, c0=0, c1=NQ):
                for c in range(c0, c1):
                    nc.gpsimd.tensor_tensor(xs[:, par, c * QT:(c + 1) * QT, 0:C], quad_f(src[:, j, :], c),
                                            kv_scale[:, c * QT:(c + 1) * QT, :].to_broadcast([P, QT, C]),
                                            ALU.mult).then_inc(s_xs, 1)

            ROOT_C = float(C) ** 0.5

            def refine(s_rstd, s_pool, s_read, par, g, width):
                r, v = rstd_c[:, par, :, 0:width], var_c[:, par, :, 0:width]
                r2, vr2, factor = (newton[:, i, :, 0:width] for i in range(3))
                pool.wait_ge(s_rstd, g + 1)
                nc.gpsimd.tensor_tensor(r2, r, r, ALU.mult).then_inc(s_pool, 1)
                pool.wait_ge(s_pool, g * 5 + 1)
                nc.gpsimd.tensor_tensor(vr2, r2, v, ALU.mult).then_inc(s_pool, 1)
                wait_alone(pool, "pool", s_pool, g * 5 + 2)
                nc.gpsimd.tensor_scalar(factor, vr2, -0.5 * ROOT_C, 1.5 * ROOT_C, ALU.mult, ALU.add).then_inc(s_pool, 1)
                pool.wait_ge(s_pool, g * 5 + 3)
                nc.gpsimd.tensor_tensor(rstd[:, :, 0:width], r, factor, ALU.mult).then_inc(s_pool, 1)
                wait_alone(pool, "pool", s_pool, g * 5 + 4)
                pool.sem_inc(s_read, 1)

            def group_a(j, par, g, first=False):
                refine(a_rstd, a_pool, a_var_read, par, g, 3)
                if not first:
                    pool.wait_ge(a_gram, (g - 1) * NQ + PRIMED)
                nc.gpsimd.tensor_tensor(kv_scale[:, :, :], rstd[:, :, 1:2], rstd[:, :, 2:3], ALU.mult)
                nc.gpsimd.tensor_copy(r1_all[:, bass.ds(g * GT, GT)], rstd[:, :, 0])
                nc.gpsimd.tensor_copy(xs[:, par, :, C:C + 2], rstd[:, :, 1:3]).then_inc(a_pool, 1)
                pool.wait_ge(a_pool, g * 5 + 5)
                scale_quads(xg, j, par, a_xs)

            def add_x(j, g):
                pool.wait_ge(b_scaled, g + 1)
                nc.gpsimd.tensor_tensor(quad_f(x2g[:, j, :], DQ), quad_f(x2g[:, j, :], DQ), quad_f(xg[:, j, :], DQ),
                                        ALU.add).then_inc(b_added, 1)

            def group_b(j, par, g):
                refine(b_rstd, b_pool, b_var_read, par, g, 1)
                pool.wait_ge(b_gram, (g - 1) * NQ + RING * NQ)
                nc.gpsimd.tensor_tensor(kv_scale[:, :, :], rstd[:, :, 0:1], rstd[:, :, 0:1], ALU.mult)
                nc.gpsimd.tensor_copy(r2_all[:, bass.ds(g * GT, GT)], rstd[:, :, 0])
                nc.gpsimd.tensor_copy(xs[:, par, :, C:C + 1], rstd[:, :, 0:1]).then_inc(b_pool, 1)
                pool.wait_ge(b_pool, g * 5 + 5)
                scale_quads(x2g, j, par, b_xs, 0, NQ - 1)
                if not (isinstance(g, int) and g == B * GB - 1):
                    add_x((j + 1) % RING, g + 1)
                scale_quads(x2g, j, par, b_xs, NQ - 1, NQ)

            group_a(0, 0, 0, first=True)
            with pool.Fori(0, B * BODIES) as n:
                g0 = pool.snap(n * RING)
                for j in range(RING):
                    group_a((j + 1) % RING, (j + 1) % 2, g0 + (j + 1))

            add_x(0, 0)
            group_b(0, 0, 0)
            with pool.Fori(0, B * BODIES - 1) as n:
                g0 = pool.snap(n * RING)
                for j in range(RING):
                    group_b((j + 1) % RING, (j + 1) % 2, g0 + (j + 1))
            for j in range(1, RING):
                group_b(j, j % 2, (B * BODIES - 1) * RING + j)

            pool.wait_ge(b_pool, 5 * B * GB)

            AHEAD = 4
            r2_by_batch = r2_all[:, :].rearrange("p (b t) -> p b t", b=B)
            x2_part = xg[:, :, :].rearrange("p l (b t c) -> p l b t c", b=B, c=C)

            def normalise(s, t, token):
                part = t // LT % PARTS
                nc.gpsimd.tensor_tensor(xn[:, t % 4, :, :], x2_part[:, part, :, t % LT, :],
                                        r2_by_batch[:, :, bass.ds(token, 1)].to_broadcast([P, B, C]), ALU.mult).then_inc(c_xn, 1)

            def body_c(n, k):
                s0 = n * BT if isinstance(n, int) else pool.snap(n * BT)
                token0 = k * BT if isinstance(k, int) else pool.snap(k * BT)
                token_next = (k + 1) % CB * BT if isinstance(k, int) else pool.snap((k + 1) % CB * BT)
                for t in range(BT):
                    ta = t + AHEAD
                    if ta % LT == 0:
                        pool.wait_ge(x2_in[ta // LT % PARTS], n * 16 + 16 * (1 + ta // BT))
                    pool.wait_ge(c_T, s0 + t + 1)
                    normalise(s0 + ta, ta, token0 + ta if ta < BT else token_next + (ta - BT))

            pool.wait_ge(x2_in[0], 16)
            for t in range(AHEAD):
                normalise(t, t, (CB - 1) * BT + t)
            body_c(0, CB - 1)
            limit = pool.alloc_register("pool_limit")
            pool.reg_mov(limit, 1)
            with pool.Fori(0, limit) as r:
                with pool.Fori(0, CB) as k:
                    body_c(r * CB + k + 1, k)
                wait_alone(pool, "pool", diff_ready, r + 1)
                nc.gpsimd.partition_all_reduce(diff_all[:, :], diff_max[:, :], P,
                                               bass.bass_isa.ReduceOp.max).then_inc(diff_reduced, 1)
                wait_alone(pool, "pool", verdict, r + 1)
                pool.reg_load(limit, rounds_limit[0:1, 0:1])


_INS = ['x', 'L0_conv_Wq', 'L0_conv_Wk', 'L0_conv_Wv', 'L0_conv_gamma_k', 'L0_conv_beta_k', 'L0_ffn_W', 'L0_ffn_V',
        'L0_ffn_gamma', 'L0_ffn_beta']
_OUTS = [((4, 256, 256, 128), 'float32')]


def kernel(**inputs):
    import numpy as _np
    import concourse.bacc as _bacc
    from concourse import mybir as _mybir
    from concourse.bass_utils import run_bass_kernel_spmd as _run

    nc = _bacc.Bacc("TRN2", target_bir_lowering=False, num_devices=1)
    arrays, args = {}, []
    for name in _INS:
        a = _np.ascontiguousarray(inputs[name])
        arrays[f"in_{name}_dram"] = a
        args.append(nc.dram_tensor(f"in_{name}_dram", a.shape, _mybir.dt.from_np(a.dtype), kind="ExternalInput").ap())
    for i, (shape, dtype) in enumerate(_OUTS):
        dt = _mybir.dt.from_np(_np.dtype(dtype))
        args.append(nc.dram_tensor(f"out_{i}_dram", shape, dt, kind="ExternalOutput").ap())
    metaformer_program(nc, *args)
    r = _run(nc, [arrays], core_ids=[0])
    got = tuple(r.results[0][f"out_{i}_dram"] for i in range(len(_OUTS)))
    return got[0]
```
